# Optimizing a Trainium2 kernel written in Bass

```python
import numpy as np
import jax
import jax.numpy as jnp

def _softmax(x, axis=-1):
    return jax.nn.softmax(x, axis=axis)

def _gelu(x):
    return jax.nn.gelu(x, approximate=True)

def _silu(x):
    return jax.nn.silu(x)

def _sigmoid(x):
    return jax.nn.sigmoid(x)

def _layernorm(x, axis=-1, eps=1e-05):
    m = jnp.mean(x, axis=axis, keepdims=True)
    v = jnp.var(x, axis=axis, keepdims=True)
    return (x - m) / jnp.sqrt(v + eps)

def _scatter_add(tgt, idx, src, axis=0):
    return tgt.at[idx].add(src)

def _segment_sum(src, seg, n):
    return jax.ops.segment_sum(src, seg, n)
kernel_name = 'mk_xattn_ffn_d1_seqx_r4_d366f7'

def setup_inputs(seed: int=0):
    np.random.seed(seed)
    _w = jnp.asarray

    def _rec_inputs():
        import jax
        import jax.numpy as jnp
        _rk = jax.random.key(seed)
        x = 0.002226 + 0.9996 * jax.random.normal(jax.random.fold_in(_rk, 1), (2, 1024, 256), jnp.float32)
        _lenS = 1024 - jax.random.randint(jax.random.fold_in(_rk, 7), (2,), 0, max(1, 1024 // 4) + 1, jnp.int32)
        _lenS2 = 77 - jax.random.randint(jax.random.fold_in(_rk, 8), (2,), 0, max(1, 77 // 4) + 1, jnp.int32)
        _ctx_1024P = jax.random.normal(jax.random.fold_in(_rk, 11), (2, 16, 256), jnp.float32)
        _ctx_1024c = jax.random.dirichlet(jax.random.fold_in(_rk, 511), 0.3 * jnp.ones((16,), jnp.float32), (2, 77))
        _ctx_1024t = jnp.einsum('bsk,bkd->bsd', _ctx_1024c, _ctx_1024P)
        _ctx_1024t = _ctx_1024t * jax.lax.rsqrt(jnp.mean(jnp.square(_ctx_1024t)) + 1e-12) * 0.953939
        ctx_1024 = -0.000125008 + 0.999885 * (_ctx_1024t + 0.3 * jax.random.normal(jax.random.fold_in(_rk, 611), (2, 77, 256), jnp.float32))
        return (x, ctx_1024)
    x, ctx_1024 = _rec_inputs()

    def _L0_xattn_setup():
        import jax, jax.numpy as jnp
        import numpy as np
        EPS = 1e-05

        def layer_norm(x, g, b):
            mu = jnp.mean(x, axis=-1, keepdims=True)
            var = jnp.var(x, axis=-1, keepdims=True)
            return (x - mu) * jax.lax.rsqrt(var + EPS) * g + b
        key = jax.random.key(seed)
        ks = jax.random.split(key, 8)
        dim, heads, dim_head = (256, 16, 64)
        inner = heads * dim_head
        b, n, m = (8, 1024, 64)
        s = dim ** (-0.5)
        return {'x': jax.random.normal(ks[0], (b, n, dim), jnp.float32), 'latents': jax.random.normal(ks[1], (b, m, dim), jnp.float32), 'ln_m_g': jnp.ones((dim,), jnp.float32), 'ln_m_b': jnp.zeros((dim,), jnp.float32), 'ln_l_g': jnp.ones((dim,), jnp.float32), 'ln_l_b': jnp.zeros((dim,), jnp.float32), 'Wq': jax.random.normal(ks[2], (dim, inner), jnp.float32) * s, 'Wkv': jax.random.normal(ks[3], (dim, 2 * inner), jnp.float32) * s, 'Wout': jax.random.normal(ks[4], (inner, dim), jnp.float32) * s}
    _L0_xattn_all = _L0_xattn_setup()
    _L0_xattn_in = {k: v for k, v in _L0_xattn_all.items() if k in ('ln_m_g', 'ln_m_b', 'ln_l_g', 'ln_l_b', 'Wq', 'Wkv', 'Wout')}
    del _L0_xattn_all

    def _L0_ffn_setup():
        import jax, jax.numpy as jnp
        import numpy as np
        B, S, D = (2, 512, 256)
        E, G, K = (32, 8, 4)
        H, SH = (512, 512)
        CAP_FACTOR = 1.25

        def _l2norm(v):
            n = jnp.linalg.norm(v, axis=-1, keepdims=True)
            return v / jnp.maximum(n, 1e-12)
        key = jax.random.key(seed)
        ks = jax.random.split(key, 10)
        x = jax.random.normal(ks[0], (B, S, D), jnp.float32)
        group_centroids = jax.random.normal(ks[1], (G, D), jnp.float32) * 0.02
        expert_centroids = jax.random.normal(ks[2], (E, D), jnp.float32) * 0.02
        bias = jnp.zeros((E,), jnp.float32)
        sd_in = 1.0 / np.sqrt(D).astype(np.float32)
        sd_h = 1.0 / np.sqrt(H).astype(np.float32)
        wg = jax.random.normal(ks[3], (E, D, H), jnp.float32) * sd_in
        wu = jax.random.normal(ks[4], (E, D, H), jnp.float32) * sd_in
        wd = jax.random.normal(ks[5], (E, H, D), jnp.float32) * sd_h
        sg = jax.random.normal(ks[6], (D, SH), jnp.float32) * sd_in
        su = jax.random.normal(ks[7], (D, SH), jnp.float32) * sd_in
        sd_w = jax.random.normal(ks[8], (SH, D), jnp.float32) * sd_h
        return dict(x=x, group_centroids=group_centroids, expert_centroids=expert_centroids, bias=bias, wg=wg, wu=wu, wd=wd, sg=sg, su=su, sd=sd_w)
    _L0_ffn_all = _L0_ffn_setup()
    _L0_ffn_in = {k: v for k, v in _L0_ffn_all.items() if k in ('group_centroids', 'expert_centroids', 'bias', 'wg', 'wu', 'wd', 'sg', 'su', 'sd')}
    del _L0_ffn_all
    return {'x': x, 'ctx_1024': ctx_1024, 'L0_xattn_ln_m_g': _L0_xattn_in['ln_m_g'], 'L0_xattn_ln_m_b': _L0_xattn_in['ln_m_b'], 'L0_xattn_ln_l_g': _L0_xattn_in['ln_l_g'], 'L0_xattn_ln_l_b': _L0_xattn_in['ln_l_b'], 'L0_xattn_Wq': _L0_xattn_in['Wq'], 'L0_xattn_Wkv': _L0_xattn_in['Wkv'], 'L0_xattn_Wout': _L0_xattn_in['Wout'], 'L0_ffn_group_centroids': _L0_ffn_in['group_centroids'], 'L0_ffn_expert_centroids': _L0_ffn_in['expert_centroids'], 'L0_ffn_bias': _L0_ffn_in['bias'], 'L0_ffn_wg': _L0_ffn_in['wg'], 'L0_ffn_wu': _L0_ffn_in['wu'], 'L0_ffn_wd': _L0_ffn_in['wd'], 'L0_ffn_sg': _L0_ffn_in['sg'], 'L0_ffn_su': _L0_ffn_in['su'], 'L0_ffn_sd': _L0_ffn_in['sd']}

def reference(x, ctx_1024, L0_xattn_ln_m_g, L0_xattn_ln_m_b, L0_xattn_ln_l_g, L0_xattn_ln_l_b, L0_xattn_Wq, L0_xattn_Wkv, L0_xattn_Wout, L0_ffn_group_centroids, L0_ffn_expert_centroids, L0_ffn_bias, L0_ffn_wg, L0_ffn_wu, L0_ffn_wd, L0_ffn_sg, L0_ffn_su, L0_ffn_sd):
    import jax
    import jax.numpy as jnp

    def _L0_xattn_ref(x, latents, ln_m_g, ln_m_b, ln_l_g, ln_l_b, Wq, Wkv, Wout):
        import jax, jax.numpy as jnp
        import numpy as np
        EPS = 1e-05

        def layer_norm(x, g, b):
            mu = jnp.mean(x, axis=-1, keepdims=True)
            var = jnp.var(x, axis=-1, keepdims=True)
            return (x - mu) * jax.lax.rsqrt(var + EPS) * g + b
        heads, dim_head = (16, 64)
        scale = dim_head ** (-0.5)
        x = layer_norm(x, ln_m_g, ln_m_b)
        lat = layer_norm(latents, ln_l_g, ln_l_b)
        b, m, _ = lat.shape
        q = lat @ Wq
        kv_input = jnp.concatenate([x, lat], axis=1)
        kv = kv_input @ Wkv
        k, v = jnp.split(kv, 2, axis=-1)

        def split_heads(t):
            return t.reshape(t.shape[0], t.shape[1], heads, dim_head).transpose(0, 2, 1, 3)
        q, k, v = (split_heads(q), split_heads(k), split_heads(v))
        dots = jnp.einsum('bhid,bhjd->bhij', q, k) * scale
        attn = jax.nn.softmax(dots, axis=-1)
        out = jnp.einsum('bhij,bhjd->bhid', attn, v)
        out = out.transpose(0, 2, 1, 3).reshape(b, m, heads * dim_head)
        return out @ Wout

    def _L0_ffn_ref(x, group_centroids, expert_centroids, bias, wg, wu, wd, sg, su, sd):
        import jax, jax.numpy as jnp
        import numpy as np
        B, S, D = (2, 512, 256)
        E, G, K = (32, 8, 4)
        H, SH = (512, 512)
        CAP_FACTOR = 1.25

        def _l2norm(v):
            n = jnp.linalg.norm(v, axis=-1, keepdims=True)
            return v / jnp.maximum(n, 1e-12)
        b, s, d = x.shape
        xf = x.reshape(-1, d)
        N = xf.shape[0]
        shared = jax.nn.silu(xf @ sg) * (xf @ su) @ sd
        xn = _l2norm(xf)
        group_scores = xn @ _l2norm(group_centroids).T
        n_top_groups = max(1, G // 2)
        _, top_group_idx = jax.lax.top_k(group_scores, n_top_groups)
        expert_scores = xn @ _l2norm(expert_centroids).T + bias
        expert_to_group = jnp.arange(E) // (E // G)
        sel = jnp.zeros((N, G), xf.dtype).at[jnp.arange(N)[:, None], top_group_idx].set(1.0)
        group_mask = sel[:, expert_to_group]
        masked = expert_scores * group_mask + (1.0 - group_mask) * -1000000000.0
        top_scores, top_idx = jax.lax.top_k(masked, K)
        gates = jax.nn.softmax(top_scores, axis=-1)
        capacity = max(1, int(N / E * K * CAP_FACTOR))
        flat_e = top_idx.reshape(-1)
        flat_g = gates.reshape(-1)
        tok = jnp.repeat(jnp.arange(N), K)
        onehot = jax.nn.one_hot(flat_e, E, dtype=jnp.int32)
        pos = jnp.cumsum(onehot, axis=0)[jnp.arange(N * K), flat_e] - 1
        keep = pos < capacity
        e_s = jnp.where(keep, flat_e, E)
        p_s = jnp.where(keep, pos, 0)
        buf = jnp.zeros((E + 1, capacity, d), xf.dtype).at[e_s, p_s].set(xf[tok])[:E]
        h = jax.nn.silu(jnp.einsum('ecd,edh->ech', buf, wg)) * jnp.einsum('ecd,edh->ech', buf, wu)
        out_e = jnp.einsum('ech,ehd->ecd', h, wd)
        gathered = out_e[flat_e, jnp.minimum(pos, capacity - 1)]
        contrib = gathered * (flat_g * keep.astype(xf.dtype))[:, None]
        routed = jnp.zeros_like(xf).at[tok].add(contrib)
        return (shared + routed).reshape(b, s, d)
    x = x + _L0_xattn_ref(ctx_1024, _layernorm(x, axis=-1), L0_xattn_ln_m_g, L0_xattn_ln_m_b, L0_xattn_ln_l_g, L0_xattn_ln_l_b, L0_xattn_Wq, L0_xattn_Wkv, L0_xattn_Wout)
    x = x + _L0_ffn_ref(_layernorm(x, axis=-1), L0_ffn_group_centroids, L0_ffn_expert_centroids, L0_ffn_bias, L0_ffn_wg, L0_ffn_wu, L0_ffn_wd, L0_ffn_sg, L0_ffn_su, L0_ffn_sd)
    return x

_drawn_inputs = setup_inputs


def setup_inputs(seed=0):
    import zlib

    import numpy as np

    out = dict(_drawn_inputs(seed))
    spreads = {'L0_xattn_ln_m_g': (1.0, 0.2),
     'L0_xattn_ln_m_b': (0.0, 0.1),
     'L0_xattn_ln_l_g': (1.0, 0.2),
     'L0_xattn_ln_l_b': (0.0, 0.1),
     'L0_ffn_bias': (0.0, 0.1)}
    factors = {}
    for name, (base, spread) in spreads.items():
        noise = np.random.default_rng([zlib.crc32(name.encode()), seed]).standard_normal(out[name].shape)
        drawn = base * np.exp(spread * noise) if base else spread * noise
        out[name] = jnp.asarray(drawn.astype(out[name].dtype))
    for name, factor in factors.items():
        out[name] = (out[name] * factor).astype(out[name].dtype)
    return out
```

```python
from contextlib import ExitStack

import concourse.bass as bass
from concourse import mybir

F32 = mybir.dt.float32
I32 = mybir.dt.int32
U32 = mybir.dt.uint32
ALU = mybir.AluOpType
ACT = mybir.ActivationFunctionType
AX = mybir.AxisListType
P = 128


class Chain:

    def __init__(self, eng, sem):
        self.eng, self.sem, self.n = eng, sem, 0

    def done(self, ins):
        self.n += 1
        ins.then_inc(self.sem, 1)

    def wait(self):
        self.eng.wait_ge(self.sem, self.n)


def xattn_moe(nc, x, ctx_in, ln_m_g, ln_m_b, ln_l_g, ln_l_b, Wq, Wkv, Wout, group_c, expert_c, e_bias,
              wg, wu, wd, sg, su, sd, out):
    B, S, D = x.shape
    CT = ctx_in.shape[1]
    INNER = Wq.shape[1]
    DH = 64
    H = INNER // DH
    HP = H // 2
    DT = D // P
    QT_N = S // P
    NT = B * QT_N
    NTOK = B * S
    KEYS = S + CT
    KT_N = QT_N + 1
    G, E = group_c.shape[0], expert_c.shape[0]
    TOPG, TOPK = G // 2, 4
    PER_G = E // G
    HID = wg.shape[2]
    HT = HID // P
    CAP = max(1, int(NTOK / E * TOPK * 1.25))
    CAP_TILES = [(c, min(P, CAP - c)) for c in range(0, CAP, P)]
    CTL = len(CAP_TILES)
    SLOTS = E * CAP
    ROWS = NTOK + CAP
    EPS = 1e-5
    GE = G + E

    JOBS_A = B * DT * 2 + DT + DT
    JOBS_B = 8 + 3 * 2 * QT_N
    JOBS_HP = B * JOBS_B
    J_WOUT = JOBS_A + HP * JOBS_HP
    J_HT = J_WOUT
    J_SHARED = J_WOUT + NT * 2 + NT // 4 * DT
    J_EXPERT = J_SHARED + NT
    assert JOBS_A % 2 == JOBS_HP % 2 == J_SHARED % 2 == J_EXPERT % 2 == 0
    UNITS = 2 * QT_N
    NCHUNK = NTOK // 512

    tbl = nc.dram_tensor("slot_table", [SLOTS + NTOK * TOPK, 2], I32, kind="Internal").ap()
    hrows = nc.dram_tensor("h_rows", [ROWS, D], F32, kind="Internal").ap()
    acc = nc.dram_tensor("acc_rows", [ROWS, D], F32, kind="Internal").ap()

    with ExitStack() as stack:
        def sb(name, shape, dt=F32):
            return stack.enter_context(nc.sbuf_tensor(name, shape, dt))

        def sem(name):
            return stack.enter_context(nc.semaphore(name))

        x_sb = sb("x_sb", [P, NT, D])
        ctx_sb = sb("ctx_sb", [CT, B, D])
        kvT = sb("kvT", [P, DT, B * KEYS])
        o_all = sb("o_all", [P, NT * INNER])
        qkv = sb("qkv", [P, B, S + KEYS + KT_N * P])
        probs = sb("probs", [P, 2, KEYS])
        probsT = sb("probsT", [P, 2, KT_N, P])
        w_hp = sb("w_hp", [P, DT, 3, P])
        wout_sb = sb("wout_sb", [P, HP, D])
        h_sb = sb("h_sb", [P, NT, D])
        ident = sb("ident", [P, P])
        lower = sb("lower", [P, P])
        ones = sb("ones", [P, P])
        zeros = sb("zeros", [P, ROWS * D // P - NTOK * D // P])
        tinit = sb("tinit", [E, CAP, 2], I32)
        gb = sb("gb", [P, 4, DT])
        eps = sb("eps", [P, 1])
        bias_bc = sb("bias_bc", [P, E])
        cen = sb("cen", [GE, D])
        cstat = sb("cstat", [GE, 4])
        cT = sb("cT", [P, DT, GE])
        stats = sb("stats", [P, NT, 6])
        mv = sb("mv", [P, NT + B, 2])
        cstats = sb("cstats", [CT, B, 6])
        std = sb("std", [P, NT + B])
        rstd = sb("rstd", [P, NT + B])
        negmax = sb("negmax", [P, 2])
        rowsum = sb("rowsum", [P, 2, 2])
        rinv = sb("rinv", [P, 2])
        ssq = sb("ssq", [P, NT])
        rnorm = sb("rnorm", [P, NT])
        sq_junk = sb("sq_junk", [P, D])
        sc = sb("sc", [P, NT, GE])
        masked = sb("masked", [P, NT, E])
        top8 = sb("top8", [P, NT, 8])
        top8i = sb("top8i", [P, NT, 8], U32)
        topf = sb("topf", [P, NT, TOPK])
        onehot = sb("onehot", [P, NT, TOPK, E])
        gmask = sb("gmask", [P, NT, G])
        chosen = sb("chosen", [P, NT, E])
        before = sb("before", [P, NT, E])
        posk = sb("posk", [P, NT, TOPK])
        keep = sb("keep", [P, NT, TOPK])
        dropslot = sb("dropslot", [P, NT, TOPK])
        slot = sb("slot", [P, NT, TOPK], I32)
        entry = sb("entry", [P, NT, TOPK, 2], I32)
        gsum = sb("gsum", [P, NT])
        iota_e = sb("iota_e", [P, E])

        z_sb = o_all[:, 0:NT * D].rearrange("p (t d) -> p t d", t=NT)
        zc_sb = o_all[0:CT, NT * D:(NT + B) * D].rearrange("p (t d) -> p t d", t=B)
        oT = probsT
        picked = probs[:, :, :].rearrange("p a n -> p (a n)")[:, 0:NT * TOPK * E]\
            .rearrange("p (t k e) -> p t k e", t=NT, k=TOPK)
        QTb = [qkv[:, b, 0:S] for b in range(B)]
        KTb = [qkv[:, b, S:S + KEYS] for b in range(B)]
        Vb = [qkv[:, b, S + KEYS:].rearrange("p (k n) -> p k n", k=KT_N) for b in range(B)]
        hT = kvT[:, :, 0:NTOK]
        flat_qkv = qkv[:, :, :].rearrange("p b n -> p (b n)")
        W = DT * HID
        sg_sb = flat_qkv[:, 0:W].rearrange("p (k n) -> p k n", k=DT)
        su_sb = flat_qkv[:, W:2 * W].rearrange("p (k n) -> p k n", k=DT)
        sd_sb = flat_qkv[:, 2 * W:3 * W].rearrange("p (k n) -> p k n", k=HT)
        shid = flat_qkv[:, 3 * W:3 * W + HT * 512].rearrange("p (k n) -> p k n", k=HT)
        sacc = flat_qkv[:, 3 * W + HT * 512:3 * W + HT * 512 + 4 * D].rearrange("p (k n) -> p k n", k=4)
        at = [0]

        def carve(words, parts=P):
            at[0] += words
            return o_all[0:parts, at[0] - words:at[0]]

        wg_sb = [carve(W).rearrange("p (k n) -> p k n", k=DT) for _ in range(2)]
        wu_sb = [carve(W).rearrange("p (k n) -> p k n", k=DT) for _ in range(2)]
        wd_sb = [carve(W).rearrange("p (k n) -> p k n", k=HT) for _ in range(2)]
        xg = [carve(CTL * D).rearrange("p (c n) -> p c n", c=CTL) for _ in range(2)]
        xeT = [carve(DT * CAP).rearrange("p (k n) -> p k n", k=DT) for _ in range(2)]
        ehid = [carve(HT * CAP).rearrange("p (k n) -> p k n", k=HT) for _ in range(2)]
        y_sb = [carve(CTL * D).rearrange("p (c n) -> p c n", c=CTL) for _ in range(2)]
        silu = [carve(512) for _ in range(2)]
        ids_g = sb("ids_g", [P, 2, CTL, 2], I32)
        ids_s = sb("ids_s", [P, 2, CTL, 2], I32)

        ps_s = stack.enter_context(nc.psum_tensor("ps_s", [P, 5 * 512], F32))
        ps_o = stack.enter_context(nc.psum_tensor("ps_o", [P, 512], F32))
        ps_t = [stack.enter_context(nc.psum_tensor(f"ps_t{i}", [P, 512], F32)) for i in range(2)]
        LAT0 = [0, 3 * 512]
        CTX0 = [2 * 512, 3 * 512 - CT]
        ROW0 = [0, 3 * 512 - CT]
        PLAT = [0, CT]
        PCTX = [S, 0]

        x_in = sem("x_in")
        small_in = sem("small_in")
        wout_in = sem("wout_in")
        w_in = sem("w_in")
        consts = sem("consts")
        dve_seq = sem("dve_seq")
        act_seq = sem("act_seq")
        pool_seq = sem("pool_seq")
        pool_step = sem("pool_step")
        var_ready = sem("var_ready")
        std_ready = sem("std_ready")
        z_ready = sem("z_ready")
        job_ready = [sem(f"job_ready{i}") for i in range(2)]
        job_free = [sem(f"job_free{i}") for i in range(2)]
        scores_ready = sem("scores_ready")
        rowmax = sem("rowmax")
        exp_done = sem("exp_done")
        o_ready = sem("o_ready")
        o_free = sem("o_free")
        rinv_ready = sem("rinv_ready")
        y_ready = sem("y_ready")
        x1_ready = sem("x1_ready")
        h_ready = sem("h_ready")
        hrows_out = sem("hrows_out")
        init_out = sem("init_out")
        norm_ready = sem("norm_ready")
        router_ready = sem("router_ready")
        chosen_ready = sem("chosen_ready")
        pos_ready = sem("pos_ready")
        gate_in = sem("gate_in")
        gate_exp = sem("gate_exp")
        slots_ready = sem("slots_ready")
        tbl_out = sem("tbl_out")
        shared_in = sem("shared_in")
        gu_ready = sem("gu_ready")
        silu_done = sem("silu_done")
        gu_free = sem("gu_free")
        sacc_out = [sem(f"sacc_out{i}") for i in range(2)]
        ew_in = [sem(f"ew_in{i}") for i in range(2)]
        idg_in = [sem(f"idg_in{i}") for i in range(2)]
        ids_in = [sem(f"ids_in{i}") for i in range(2)]
        rows_in = [sem(f"rows_in{i}") for i in range(2)]
        ey_ready = sem("ey_ready")
        ysb_ready = sem("ysb_ready")
        ysb_free = sem("ysb_free")
        add_out = sem("add_out")
        final_out = sem("final_out")

        def bank_free(eng, j, more=0):
            eng.wait_ge(job_free[j % 2], j // 2 + 1 + more)

        def job_done(eng, j, more=0):
            eng.wait_ge(job_free[j % 2], j // 2 + 2 + more)

        def job_filled(eng, j, more=0):
            eng.wait_ge(job_ready[j % 2], j // 2 + 1 + more)

        block = stack.enter_context(nc.Block())

        @block.sync
        def _(sp):
            for b in range(B):
                sp.dma_start(x_sb[:, b * QT_N:(b + 1) * QT_N, :],
                             x[b].rearrange("(t p) d -> p t d", p=P)).then_inc(x_in, 16)
            sp.dma_start(ctx_sb[:, :, :], ctx_in.rearrange("b t d -> t b d")).then_inc(small_in, 16)
            for i, v in enumerate((ln_l_g, ln_l_b, ln_m_g, ln_m_b)):
                sp.dma_start(gb[:, i, :], v.rearrange("(k p) -> p k", p=P), allow_slow_non_contiguous=True).then_inc(small_in, 16)
            sp.dma_start(bias_bc[:, :], e_bias.partition_broadcast(P)).then_inc(small_in, 16)
            sp.dma_start(cen[0:G, :], group_c).then_inc(small_in, 16)
            sp.dma_start(cen[G:GE, :], expert_c).then_inc(small_in, 16)
            sp.dma_start(wout_sb[:, :, :], Wout.rearrange("(h p) n -> p h n", p=P)).then_inc(wout_in, 16)
            sp.wait_ge(consts, 2)
            for t in (hrows, acc):
                sp.dma_start(t[NTOK:ROWS, :].rearrange("r d -> (r d)").rearrange("(p n) -> p n", p=P),
                             zeros[:, :]).then_inc(init_out, 16)
            sp.dma_start(tbl[0:SLOTS, :].rearrange("(e c) w -> e (c w)", e=E),
                         tinit[:, :, :].rearrange("e c w -> e (c w)")).then_inc(init_out, 16)

            def load_pair(hp):
                for i, (w, col) in enumerate(((Wq, 0), (Wkv, 0), (Wkv, INNER))):
                    sp.dma_start(w_hp[:, :, i, :],
                                 w[:, bass.ds(hp * P + col, P)].rearrange("(k p) n -> p k n", p=P))\
                      .then_inc(w_in, 16)

            load_pair(0)
            with sp.Fori(0, HP - 1) as hp:
                job_filled(sp, JOBS_A + (B - 1) * JOBS_B + 7, hp * (JOBS_HP // 2))
                load_pair(hp + 1)
            job_filled(sp, J_WOUT)
            for dst, w in ((sg_sb, sg), (su_sb, su), (sd_sb, sd)):
                sp.dma_start(dst, w.rearrange("(k p) n -> p k n", p=P)).then_inc(shared_in, 16)
            for g in range(NT // 4):
                sp.wait_ge(h_ready, g + 1)
                sp.dma_start(hrows[g * 4 * P:(g + 1) * 4 * P, :].rearrange("(t p) d -> p t d", p=P),
                             h_sb[:, g * 4:(g + 1) * 4, :]).then_inc(hrows_out, 16)
            with sp.Fori(0, NCHUNK) as c:
                for half in range(2):
                    for i in range(2):
                        job_done(sp, J_SHARED + half * 2 + i, c * 2)
                    sp.dma_start(acc[bass.ds(c * 512 + half * 256, 256), :].rearrange("(t p) d -> p t d", p=P),
                                 sacc[:, half * 2:half * 2 + 2, :]).then_inc(sacc_out[half], 16)
            sp.wait_ge(tbl_out, 16 * NT * TOPK)
            sp.wait_ge(x1_ready, NT)
            with sp.Fori(0, E // 2) as i:
                for par in range(2):
                    e = i * 2 + par
                    sp.wait_ge(job_ready[1], (J_EXPERT // 2 - 2 + 1) + e)
                    sp.dma_start(ids_g[:, par, 0:CTL - 1, :],
                                 tbl[bass.ds(e * CAP, (CTL - 1) * P), :].rearrange("(c p) w -> p c w", p=P))\
                      .then_inc(idg_in[par], 16)
                    sp.dma_start(ids_g[0:CAP_TILES[-1][1], par, CTL - 1, :],
                                 tbl[bass.ds(e * CAP + (CTL - 1) * P, CAP_TILES[-1][1]), :]).then_inc(idg_in[par], 16)
                    sp.wait_ge(ey_ready, e * CTL + CTL)
                    for dst, w in ((wg_sb, wg), (wu_sb, wu), (wd_sb, wd)):
                        sp.dma_start(dst[par], w[bass.ds(e, 1)].rearrange("o (k p) n -> p (o k) n", p=P))\
                          .then_inc(ew_in[par], 16)
                    sp.wait_ge(ysb_free, e + 1)
                    sp.dma_start(ids_s[:, par, 0:CTL - 1, :],
                                 tbl[bass.ds(e * CAP, (CTL - 1) * P), :].rearrange("(c p) w -> p c w", p=P))\
                      .then_inc(ids_in[par], 16)
                    sp.dma_start(ids_s[0:CAP_TILES[-1][1], par, CTL - 1, :],
                                 tbl[bass.ds(e * CAP + (CTL - 1) * P, CAP_TILES[-1][1]), :]).then_inc(ids_in[par], 16)
            sp.wait_ge(add_out, 16 * CTL * E)
            sp.dma_start(out.rearrange("b s d -> (b s) d"), acc[0:NTOK, :]).then_inc(final_out, 16)
            sp.wait_ge(final_out, 16)

        @block.gpsimd
        def _(pool):
            seq = Chain(pool, pool_seq)
            seq.done(pool.memset(zeros[:, :], 0.0))
            seq.done(pool.memset(tinit[:, :, :].bitcast(F32), 0.0))
            seq.done(pool.memset(ident[:, :], 0.0))
            seq.done(pool.memset(lower[:, :], 1.0))
            seq.done(pool.memset(ones[:, :], 1.0))
            seq.done(pool.memset(eps[:, :], EPS))
            seq.wait()
            seq.done(pool.iota(tinit[:, :, 0], pattern=[[1, CAP]], base=NTOK, channel_multiplier=0))
            seq.done(pool.affine_select(out=ident[:, :], in_=ident[:, :], compare_op=ALU.not_equal, fill=1.0,
                                        base=0, pattern=[[-1, P]], channel_multiplier=1))
            seq.done(pool.affine_select(out=lower[:, :], in_=lower[:, :], compare_op=ALU.is_gt, fill=0.0,
                                        base=0, pattern=[[1, P]], channel_multiplier=-1))
            seq.done(pool.iota(iota_e[:, :], pattern=[[1, E]], base=0, channel_multiplier=0,
                               allow_small_or_imprecise_dtypes=True))
            seq.done(pool.iota(dropslot[:, :, :], pattern=[[P * TOPK, NT], [1, TOPK]], base=SLOTS,
                               channel_multiplier=TOPK, allow_small_or_imprecise_dtypes=True))
            for k in range(TOPK):
                seq.done(pool.iota(entry[:, :, k, 0], pattern=[[P, NT]], base=0, channel_multiplier=1))
            seq.wait()
            pool.sem_inc(consts, 2)
            pool.sem_inc(ysb_free, 2)
            pool.wait_ge(init_out, 48)
            pool.wait_ge(slots_ready, 1)
            for t in range(NT):
                for k in range(TOPK):
                    pool.indirect_dma_start(
                        out=tbl[:, :], out_offset=bass.IndirectOffsetOnAxis(ap=slot[:, t, k:k + 1].bitcast(U32), axis=0),
                        in_=entry[:, t, k, :], in_offset=None).then_inc(tbl_out, 16)

            def gather(par, turn):
                pool.wait_ge(hrows_out, 16 * (NT // 4))
                pool.wait_ge(idg_in[par], turn * 32 + 32)
                pool.sem_inc(pool_step, 1)
                for c, (_, rows) in enumerate(CAP_TILES):
                    pool.indirect_dma_start(
                        out=xg[par][0:rows, c, :], out_offset=None, in_=hrows[:, :],
                        in_offset=bass.IndirectOffsetOnAxis(ap=ids_g[0:rows, par, c, 0:1].bitcast(U32), axis=0))\
                        .then_inc(rows_in[par], 16)

            def add(par, turn):
                e = turn * 2 + par
                pool.wait_ge(sacc_out[0], 16 * NCHUNK + 16)
                pool.wait_ge(sacc_out[1], 16 * NCHUNK + 16)
                pool.wait_ge(ysb_ready, e * CTL + CTL + 2)
                pool.sem_inc(pool_step, 1)
                for c, (_, rows) in enumerate(CAP_TILES):
                    pool.indirect_dma_start(
                        out=acc[:, :], in_=y_sb[par][0:rows, c, :], in_offset=None, compute_op=ALU.add,
                        out_offset=bass.IndirectOffsetOnAxis(ap=ids_s[0:rows, par, c, 0:1].bitcast(U32), axis=0))\
                        .then_inc(add_out, 16)
                pool.wait_ge(add_out, (e + 1) * 16 * CTL)
                pool.sem_inc(ysb_free, 1)

            gather(0, 0)
            with pool.Fori(0, E // 2 - 1) as i:
                gather(1, i)
                add(0, i)
                gather(0, i + 1)
                add(1, i)
            gather(1, E // 2 - 1)
            add(0, E // 2 - 1)
            add(1, E // 2 - 1)

        @block.tensor
        def _(pe):
            pe.sem_inc(ey_ready, 2 * CTL)
            pe.wait_ge(consts, 2)
            j = 0
            for b in range(B):
                pe.wait_ge(z_ready, b + 1)
                for k in range(DT):
                    for half in range(2):
                        bank_free(pe, j)
                        for i in range(4):
                            mm = pe.transpose(ps_t[j % 2][:, i * P:(i + 1) * P],
                                              z_sb[:, b * QT_N + half * 4 + i, k * P:(k + 1) * P], ident[:, :])
                        mm.then_inc(job_ready[j % 2], 1)
                        j += 1
            pe.wait_ge(z_ready, B + 1)
            for k in range(DT):
                bank_free(pe, j)
                for b in range(B):
                    mm = pe.transpose(ps_t[j % 2][:, b * P:b * P + CT], zc_sb[:, b, k * P:(k + 1) * P],
                                      ident[0:CT, 0:CT])
                mm.then_inc(job_ready[j % 2], 1)
                j += 1
            pe.wait_ge(z_ready, B + 2)
            for k in range(DT):
                bank_free(pe, j)
                pe.transpose(ps_t[j % 2][:, 0:GE], cen[:, k * P:(k + 1) * P], ident[0:GE, 0:GE])\
                  .then_inc(job_ready[j % 2], 1)
                j += 1
            assert j == JOBS_A
            job_done(pe, j - 2)
            job_done(pe, j - 1)

            with pe.Fori(0, HP) as hp:
                more = hp * (JOBS_HP // 2)
                for b in range(B):
                    j0 = JOBS_A + b * JOBS_B
                    n0 = hp * (B * UNITS) + b * UNITS

                    def project(i, col, lo, w):
                        bank_free(pe, j0 + i, more)
                        for k in range(DT):
                            mm = pe.matmul(ps_t[(j0 + i) % 2][:, 0:w], w_hp[:, k, col, :],
                                           kvT[:, k, b * KEYS + lo:b * KEYS + lo + w],
                                           start=(k == 0), stop=(k == DT - 1))
                        mm.then_inc(job_ready[(j0 + i) % 2], 1)

                    def values(i, tiles):
                        bank_free(pe, j0 + i, more)
                        for s, t in enumerate(tiles):
                            rows = P if t < QT_N else CT
                            for k in range(DT):
                                mm = pe.matmul(ps_t[(j0 + i) % 2][0:rows, s * P:(s + 1) * P],
                                               kvT[:, k, b * KEYS + t * P:b * KEYS + t * P + rows],
                                               w_hp[:, k, 2, :], start=(k == 0), stop=(k == DT - 1))
                        mm.then_inc(job_ready[(j0 + i) % 2], 1)

                    def score(u, lo, w, at):
                        qt, h = divmod(u, 2)
                        r = slice(h * DH, (h + 1) * DH)
                        return pe.matmul(ps_s[:, at:at + w], QTb[b][r, qt * P:(qt + 1) * P],
                                         KTb[b][r, lo:lo + w], start=True, stop=True)

                    def s_lat(u, half):
                        if u < UNITS:
                            score(u, half * 512, 512, LAT0[u % 2] + half * 512)

                    def s_ctx(u):
                        if u < UNITS:
                            score(u, S, CT, CTX0[u % 2]).then_inc(scores_ready, 1)

                    def t_chunk(u, c):
                        i = j0 + 8 + u * 3 + c
                        bank_free(pe, i, more)
                        for s, t in enumerate(((0, 1, 2, 3), (4, 5, 6, 7), (8,))[c]):
                            lo, rows = (PLAT[u % 2] + t * P, P) if t < QT_N else (PCTX[u % 2], CT)
                            mm = pe.transpose(ps_t[i % 2][0:rows, s * P:(s + 1) * P],
                                              probs[:, u % 2, lo:lo + rows], ident[:, :])
                        mm.then_inc(job_ready[i % 2], 1)

                    def av_chunk(u, c):
                        job_done(pe, j0 + 8 + u * 3 + c, more)
                        h = u % 2
                        for t in ((0, 1, 2, 3), (4, 5, 6, 7), (8,))[c]:
                            rows = P if t < QT_N else CT
                            mm = pe.matmul(ps_o[:, h * DH:(h + 1) * DH], probsT[0:rows, h, t, :],
                                           Vb[b][0:rows, t, h * DH:(h + 1) * DH],
                                           start=(t == 0), stop=(t == KT_N - 1))
                        return mm

                    if b == 0:
                        pe.wait_ge(w_in, hp * 48 + 48)
                    project(0, 1, 0, 512)
                    project(1, 1, 512, 512)
                    project(2, 1, S, CT)
                    project(3, 0, 0, 512)
                    project(4, 0, 512, 512)
                    values(5, range(0, 4))
                    job_done(pe, j0 + 3, more)
                    job_done(pe, j0 + 4, more)
                    s_lat(0, 0)
                    s_lat(0, 1)
                    s_ctx(0)
                    values(6, range(4, 8))
                    s_lat(1, 0)
                    s_lat(1, 1)
                    values(7, range(8, 9))
                    for u in range(UNITS):
                        pe.wait_ge(exp_done, n0 + u + 1)
                        s_ctx(u + 1)
                        t_chunk(u, 0)
                        s_lat(u + 2, 0)
                        t_chunk(u, 1)
                        s_lat(u + 2, 1)
                        if u % 2 == 0:
                            pe.wait_ge(o_free, hp * (B * QT_N) + b * QT_N + u // 2 + 1)
                        if u == 0:
                            job_done(pe, j0 + 7, more)
                        av_chunk(u, 0)
                        t_chunk(u, 2)
                        av_chunk(u, 1)
                        mm = av_chunk(u, 2)
                        if u % 2:
                            mm.then_inc(o_ready, 1)

            pe.wait_ge(o_free, HP * NT + 1)
            pe.wait_ge(wout_in, 16)
            j = J_WOUT

            def turn_o(t):
                nonlocal j
                for half in range(2):
                    bank_free(pe, j)
                    for i in range(4):
                        c = t * INNER + (half * 4 + i) * P
                        mm = pe.transpose(ps_t[j % 2][:, i * P:(i + 1) * P], o_all[:, c:c + P], ident[:, :])
                    mm.then_inc(job_ready[j % 2], 1)
                    j += 1

            def turn_h(g):
                nonlocal j
                pe.wait_ge(h_ready, g + 1)
                for k in range(DT):
                    bank_free(pe, j)
                    for i in range(4):
                        mm = pe.transpose(ps_t[j % 2][:, i * P:(i + 1) * P],
                                          h_sb[:, g * 4 + i, k * P:(k + 1) * P], ident[:, :])
                    mm.then_inc(job_ready[j % 2], 1)
                    j += 1

            turn_o(0)
            for t in range(NT):
                done = j
                if t + 1 < NT:
                    turn_o(t + 1)
                job_done(pe, done - 2 if t % 4 != 0 or t == 0 else done - 2)
                job_done(pe, done - 1)
                if t >= 2:
                    pe.wait_ge(x1_ready, t - 1)
                for k in range(HP):
                    mm = pe.matmul(ps_s[:, (t % 2) * 512:(t % 2) * 512 + D], oT[:, t % 2, k, :], wout_sb[:, k, :],
                                   start=(k == 0), stop=(k == HP - 1))
                mm.then_inc(y_ready, 1)
            for g in range(NT // 4):
                turn_h(g)
            assert j == J_SHARED
            job_done(pe, j - 2)
            job_done(pe, j - 1)
            router_bank = (ps_s[:, 2 * 512:3 * 512], ps_o)
            for t in range(NT):
                lo = (t % 8) * GE
                for k in range(DT):
                    mm = pe.matmul(router_bank[t // 8][:, lo:lo + GE], hT[:, k, t * P:(t + 1) * P], cT[:, k, :],
                                   start=(k == 0), stop=(k == DT - 1))
            mm.then_inc(router_ready, 1)
            pe.wait_ge(chosen_ready, 1)
            pe.matmul(ps_o[:, :], lower[:, :], chosen[:, :, :].rearrange("p t e -> p (t e)"), start=True, stop=False)
            pe.matmul(ps_o[:, :], ones[:, :], before[:, :, :].rearrange("p t e -> p (t e)"), start=False, stop=True)\
              .then_inc(pos_ready, 1)

            pe.wait_ge(x1_ready, NT)
            pe.wait_ge(shared_in, 48)
            with pe.Fori(0, NCHUNK) as c:
                for ht in range(HT):
                    pe.wait_ge(gu_free, c * HT + ht + 1)
                    for w, bank in ((sg_sb, 0), (su_sb, 3)):
                        at_ = (bank + ht % 2) * 512
                        for k in range(DT):
                            mm = pe.matmul(ps_s[:, at_:at_ + 512], w[:, k, ht * P:(ht + 1) * P],
                                           kvT[:, k, bass.ds(c * 512, 512)], start=(k == 0), stop=(k == DT - 1))
                    mm.then_inc(gu_ready, 1)
                for i in range(4):
                    jj = J_SHARED + i
                    bank_free(pe, jj, c * 2)
                    if i == 0:
                        pe.wait_ge(gu_free, c * HT + HT + 2)
                    for k in range(HT):
                        mm = pe.matmul(ps_t[jj % 2][:, 0:D], shid[:, k, i * P:(i + 1) * P], sd_sb[:, k, :],
                                       start=(k == 0), stop=(k == HT - 1))
                    mm.then_inc(job_ready[jj % 2], 1)

            def turn_rows(par, turn):
                pe.wait_ge(rows_in[par], turn * (16 * CTL) + 16 * CTL)
                for k in range(DT):
                    jj = J_EXPERT + par * DT + k
                    bank_free(pe, jj, turn * DT)
                    for c, (lo, rows) in enumerate(CAP_TILES):
                        mm = pe.transpose(ps_t[jj % 2][:, lo:lo + rows], xg[par][0:rows, c, k * P:(k + 1) * P],
                                          ident[0:rows, 0:rows])
                    mm.then_inc(job_ready[jj % 2], 1)

            def up(par, turn):
                g0 = NCHUNK * HT + turn * (2 * HT) + par * HT
                pe.wait_ge(ew_in[par], turn * 48 + 48)
                for k in range(DT):
                    job_done(pe, J_EXPERT + par * DT + k, turn * DT)
                for ht in range(HT):
                    pe.wait_ge(gu_free, g0 + ht + 1)
                    for w, bank in ((wg_sb, 0), (wu_sb, 3)):
                        at_ = (bank + ht % 2) * 512
                        for k in range(DT):
                            mm = pe.matmul(ps_s[:, at_:at_ + CAP], w[par][:, k, ht * P:(ht + 1) * P],
                                           xeT[par][:, k, :], start=(k == 0), stop=(k == DT - 1))
                    mm.then_inc(gu_ready, 1)

            ey_bank = (ps_o, ps_s[:, 2 * 512:3 * 512])

            def down(par, turn):
                g0 = NCHUNK * HT + turn * (2 * HT) + par * HT
                y0 = turn * (2 * CTL) + par * CTL
                pe.wait_ge(gu_free, g0 + HT + 2)
                for c, (lo, rows) in enumerate(CAP_TILES):
                    bank = ey_bank[(par * CTL + c) % 2]
                    pe.wait_ge(ysb_ready, y0 + c + 1)
                    for k in range(HT):
                        mm = pe.matmul(bank[0:rows, 0:D], ehid[par][:, k, lo:lo + rows], wd_sb[par][:, k, :],
                                       start=(k == 0), stop=(k == HT - 1))
                    mm.then_inc(ey_ready, 1)

            turn_rows(0, 0)
            with pe.Fori(0, E // 2 - 1) as i:
                up(0, i)
                turn_rows(1, i)
                down(0, i)
                up(1, i)
                turn_rows(0, i + 1)
                down(1, i)
            last = E // 2 - 1
            up(0, last)
            turn_rows(1, last)
            down(0, last)
            up(1, last)
            down(1, last)

        @block.vector
        def _(dve):
            seq = Chain(dve, dve_seq)
            for s in job_free:
                dve.sem_inc(s, 1)
            dve.sem_inc(o_free, 1)
            dve.sem_inc(gu_free, 2)
            for s in sacc_out:
                dve.sem_inc(s, 16)

            def spread(src, sts, lo, n, rows=P):
                for t in range(n):
                    seq.done(dve.bn_stats(sts[0:rows, t, :], src[0:rows, t, :]))
                seq.wait()
                for t in range(n):
                    ins = dve.bn_aggr(mv[0:rows, lo + t, :], sts[0:rows, t, :])
                    seq.done(ins)
                seq.wait()

            def normed(dst, src, lo, n, rows=P):
                seq.done(dve.reciprocal(rstd[0:rows, lo:lo + n], std[0:rows, lo:lo + n]))
                seq.wait()
                for t in range(n):
                    seq.done(dve.tensor_scalar(dst[0:rows, t, :], src[0:rows, t, :], mv[0:rows, lo + t, 0:1],
                                               rstd[0:rows, lo + t:lo + t + 1], ALU.subtract, ALU.mult))
                seq.wait()

            nv = 0
            for b in range(B):
                lo = b * QT_N
                zb = z_sb[:, lo:lo + QT_N, :]
                dve.wait_ge(x_in, 16 * B)
                for src in (x_sb[:, lo:lo + QT_N, :], zb):
                    spread(src, stats, lo, QT_N)
                    dve.sem_inc(var_ready, 1)
                    nv += 1
                    dve.wait_ge(std_ready, nv)
                    normed(zb, src, lo, QT_N)
                dve.sem_inc(z_ready, 1)
                for k in range(DT):
                    for half in range(2):
                        jj = b * DT * 2 + k * 2 + half
                        if b == 0 and k == 0 and half == 0:
                            dve.wait_ge(small_in, 16 * 8)
                        job_filled(dve, jj)
                        dve.tensor_scalar(kvT[:, k, b * KEYS + half * 512:b * KEYS + half * 512 + 512],
                                          ps_t[jj % 2][:, :], gb[:, 0, k:k + 1], gb[:, 1, k:k + 1],
                                          ALU.mult, ALU.add).then_inc(job_free[jj % 2], 1)
            spread(ctx_sb, cstats, NT, B, CT)
            dve.sem_inc(var_ready, 1)
            nv += 1
            dve.wait_ge(std_ready, nv)
            normed(zc_sb, ctx_sb, NT, B, CT)
            dve.sem_inc(z_ready, 1)
            for k in range(DT):
                jj = B * DT * 2 + k
                job_filled(dve, jj)
                dve.tensor_scalar(kvT[:, k, :].rearrange("p (b n) -> p b n", b=B)[:, :, S:KEYS],
                                  ps_t[jj % 2][:, 0:B * P].rearrange("p (b n) -> p b n", b=B)[:, :, 0:CT],
                                  gb[:, 2, k:k + 1], gb[:, 3, k:k + 1], ALU.mult, ALU.add)\
                   .then_inc(job_free[jj % 2], 1)
            dve.wait_ge(std_ready, nv + 1)
            seq.done(dve.tensor_scalar(cstat[:, 2:3], cstat[:, 1:2], 1e-12, None, ALU.max))
            seq.wait()
            seq.done(dve.reciprocal(cstat[:, 3:4], cstat[:, 2:3]))
            seq.wait()
            seq.done(dve.tensor_scalar(cen[:, :], cen[:, :], cstat[:, 3:4], None, ALU.mult))
            seq.wait()
            dve.sem_inc(z_ready, 1)
            for k in range(DT):
                jj = B * DT * 2 + DT + k
                job_filled(dve, jj)
                dve.tensor_copy(cT[:, k, :], ps_t[jj % 2][:, 0:GE]).then_inc(job_free[jj % 2], 1)

            with dve.Fori(0, HP) as hp:
                more = hp * (JOBS_HP // 2)
                for b in range(B):
                    j0 = JOBS_A + b * JOBS_B
                    n0 = hp * (B * UNITS) + b * UNITS

                    def row_max(u):
                        dve.wait_ge(scores_ready, n0 + u + 1)
                        dve.tensor_reduce(negmax[:, u % 2:u % 2 + 1], ps_s[:, ROW0[u % 2]:ROW0[u % 2] + KEYS],
                                          AX.X, ALU.max, negate=True).then_inc(rowmax, 1)

                    def out_of(i, dst, src):
                        job_filled(dve, j0 + i, more)
                        dve.tensor_copy(dst, src).then_inc(job_free[(j0 + i) % 2], 1)

                    bank = [ps_t[(j0 + i) % 2] for i in range(8)]
                    out_of(0, KTb[b][:, 0:512], bank[0][:, :])
                    out_of(2, KTb[b][:, S:KEYS], bank[2][:, 0:CT])
                    job_filled(dve, j0 + 4, more)
                    dve.tensor_scalar(QTb[b][:, 512:1024], bank[4][:, :], DH ** -0.5, None, ALU.mult)\
                       .then_inc(job_free[(j0 + 4) % 2], 1)
                    row_max(0)
                    out_of(6, Vb[b][:, 4:8, :].rearrange("p k n -> p (k n)"), bank[6][:, :])
                    for u in range(UNITS):
                        if u + 1 < UNITS:
                            row_max(u + 1)
                        i = 8 + u * 3 + 1
                        out_of(i, probsT[:, u % 2, 4:8, :].rearrange("p k n -> p (k n)"), ps_t[(j0 + i) % 2][:, :])
                        if u % 2:
                            pair = hp * (B * QT_N) + b * QT_N + u // 2
                            dve.wait_ge(o_ready, pair + 1)
                            dve.reciprocal(rinv[:, :], rowsum[:, (u // 2) % 2, :]).then_inc(rinv_ready, 1)
                            dve.wait_ge(rinv_ready, pair + 1)
                            dve.tensor_tensor(
                                o_all[:, bass.ds(hp * P + (b * QT_N + u // 2) * INNER, P)]
                                .rearrange("p (h n) -> p h n", h=2),
                                ps_o[:, 0:P].rearrange("p (h n) -> p h n", h=2),
                                rinv[:, :].unsqueeze(2).broadcast_to([P, 2, DH]), ALU.mult).then_inc(o_free, 1)

            dve.wait_ge(wout_in, 16)
            jj = J_WOUT
            for t in range(NT):
                job_filled(dve, jj + 1)
                dve.tensor_copy(oT[:, t % 2, 4:8, :].rearrange("p k n -> p (k n)"), ps_t[(jj + 1) % 2][:, :])\
                   .then_inc(job_free[(jj + 1) % 2], 1)
                jj += 2
                if t >= 1:
                    dve.wait_ge(y_ready, t)
                    dve.tensor_tensor(x_sb[:, t - 1, :], ps_s[:, ((t - 1) % 2) * 512:((t - 1) % 2) * 512 + D],
                                      x_sb[:, t - 1, :], ALU.add).then_inc(x1_ready, 1)
            dve.wait_ge(y_ready, NT)
            dve.tensor_tensor(x_sb[:, NT - 1, :], ps_s[:, 512:512 + D], x_sb[:, NT - 1, :], ALU.add).then_inc(x1_ready, 1)
            dve.wait_ge(x1_ready, NT)
            for g in range(NT // 4):
                lo = g * 4
                spread(x_sb[:, lo:lo + 4, :], stats[:, lo:lo + 4, :], lo, 4)
                dve.sem_inc(var_ready, 1)
            for g in range(NT // 4):
                lo = g * 4
                dve.wait_ge(std_ready, nv + 1 + g + 1)
                normed(h_sb[:, lo:lo + 4, :], x_sb[:, lo:lo + 4, :], lo, 4)
                dve.sem_inc(h_ready, 1)
            for g in range(NT // 4):
                for k in range(DT):
                    if k == 0:
                        job_filled(dve, jj)
                        dve.tensor_copy(hT[:, k, g * 512:(g + 1) * 512], ps_t[jj % 2][:, :])\
                           .then_inc(job_free[jj % 2], 1)
                    jj += 1
            dve.wait_ge(norm_ready, 1)
            seq.done(dve.tensor_scalar(rnorm[:, :], rnorm[:, :], 1e-12, None, ALU.max))
            seq.wait()
            seq.done(dve.reciprocal(ssq[:, :], rnorm[:, :]))
            seq.wait()
            dve.wait_ge(router_ready, 1)
            for half, bank in enumerate((ps_s[:, 2 * 512:2 * 512 + 8 * GE], ps_o[:, 0:8 * GE])):
                seq.done(dve.tensor_tensor(sc[:, half * 8:half * 8 + 8, :],
                                           bank.rearrange("p (t g) -> p t g", t=8),
                                           ssq[:, half * 8:half * 8 + 8].unsqueeze(2).broadcast_to([P, 8, GE]),
                                           ALU.mult))
            seq.wait()

            def top4(src, width):
                for t in range(NT):
                    seq.done(dve.max(top8[:, t, :], src[:, t, 0:width]))
                seq.wait()
                for t in range(NT):
                    seq.done(dve.max_index(top8i[:, t, :], top8[:, t, :], src[:, t, 0:width]))
                seq.wait()
                seq.done(dve.tensor_copy(topf[:, :, :], top8i[:, :, 0:TOPK]))
                seq.wait()

            def hot(dst, width):
                seq.done(dve.tensor_tensor(dst, topf[:, :, :].unsqueeze(3).broadcast_to([P, NT, TOPK, width]),
                                           iota_e[:, 0:width].unsqueeze(1).unsqueeze(1)
                                           .broadcast_to([P, NT, TOPK, width]), ALU.is_equal))
                seq.wait()

            dve.wait_ge(consts, 2)
            top4(sc, G)
            gh = picked[:, :, :, 0:G]
            hot(gh, G)
            seq.done(dve.tensor_reduce(gmask[:, :, :], gh.rearrange("p t k g -> p t g k"), AX.X, ALU.add))
            seq.done(dve.tensor_tensor(sc[:, :, G:GE], sc[:, :, G:GE],
                                       bias_bc[:, :].unsqueeze(1).broadcast_to([P, NT, E]), ALU.add))
            seq.wait()
            m4 = masked[:, :, :].rearrange("p t (g i) -> p t g i", i=PER_G)
            seq.done(dve.tensor_tensor(m4, sc[:, :, G:GE].rearrange("p t (g i) -> p t g i", i=PER_G),
                                       gmask[:, :, :].unsqueeze(3).broadcast_to([P, NT, G, PER_G]), ALU.mult))
            seq.wait()
            seq.done(dve.tensor_scalar(gmask[:, :, :], gmask[:, :, :], -1.0, 1e9, ALU.add, ALU.mult))
            seq.wait()
            seq.done(dve.tensor_tensor(m4, m4, gmask[:, :, :].unsqueeze(3).broadcast_to([P, NT, G, PER_G]), ALU.add))
            seq.wait()
            top4(masked, E)
            seq.done(dve.tensor_tensor(keep[:, :, :], top8[:, :, 0:TOPK], top8[:, :, 0:1].broadcast_to([P, NT, TOPK]),
                                       ALU.subtract))
            seq.wait()
            dve.sem_inc(gate_in, 1)
            hot(onehot[:, :, :, :], E)
            seq.done(dve.tensor_reduce(chosen[:, :, :], onehot[:, :, :, :].rearrange("p t k e -> p t e k"),
                                       AX.X, ALU.add))
            seq.done(dve.memset(before[:, 0, :], 0.0))
            seq.wait()
            for t in range(1, NT):
                seq.done(dve.tensor_tensor(before[:, t, :], before[:, t - 1, :], chosen[:, t - 1, :], ALU.add))
                seq.wait()
            dve.sem_inc(chosen_ready, 1)
            dve.wait_ge(gate_exp, 1)
            seq.done(dve.tensor_reduce(gsum[:, :], posk[:, :, :], AX.X, ALU.add))
            seq.wait()
            seq.done(dve.reciprocal(gsum[:, :], gsum[:, :]))
            seq.wait()
            seq.done(dve.tensor_tensor(entry[:, :, :, 1].bitcast(F32), posk[:, :, :],
                                       gsum[:, :].unsqueeze(2).broadcast_to([P, NT, TOPK]), ALU.mult))
            seq.wait()
            dve.wait_ge(pos_ready, 1)
            seq.done(dve.tensor_tensor(picked[:, :, :, :], onehot[:, :, :, :],
                                       ps_o[:, :].rearrange("p (t e) -> p t e", t=NT).unsqueeze(2)
                                       .broadcast_to([P, NT, TOPK, E]), ALU.mult))
            seq.wait()
            seq.done(dve.tensor_reduce(posk[:, :, :], picked[:, :, :, :], AX.X, ALU.add))
            seq.wait()
            seq.done(dve.tensor_scalar(keep[:, :, :], posk[:, :, :], float(CAP), None, ALU.is_lt))
            seq.done(dve.tensor_scalar(topf[:, :, :], topf[:, :, :], float(CAP), None, ALU.mult))
            seq.wait()
            seq.done(dve.tensor_tensor(posk[:, :, :], posk[:, :, :], topf[:, :, :], ALU.add))
            seq.wait()
            seq.done(dve.tensor_tensor(posk[:, :, :], posk[:, :, :], dropslot[:, :, :], ALU.subtract))
            seq.wait()
            seq.done(dve.tensor_tensor(posk[:, :, :], posk[:, :, :], keep[:, :, :], ALU.mult))
            seq.wait()
            seq.done(dve.tensor_tensor(slot[:, :, :], posk[:, :, :], dropslot[:, :, :], ALU.add))
            seq.wait()
            dve.sem_inc(slots_ready, 1)

            def hidden(dst, n, g, width):
                dve.wait_ge(silu_done, g + 1)
                dve.tensor_tensor(dst, silu[n % 2][:, 0:width], ps_s[:, (3 + n % 2) * 512:(3 + n % 2) * 512 + width],
                                  ALU.mult).then_inc(gu_free, 1)

            with dve.Fori(0, NCHUNK) as c:
                for ht in range(HT):
                    hidden(shid[:, ht, :], ht, c * HT + ht, 512)
                for i in range(4):
                    jn = J_SHARED + i
                    job_filled(dve, jn, c * 2)
                    if i % 2 == 0:
                        dve.wait_ge(sacc_out[i // 2], c * 16 + 16)
                    dve.tensor_tensor(sacc[:, i, :], ps_t[jn % 2][:, 0:D],
                                      x_sb[:, bass.ds(c * 4 + i, 1), :].rearrange("p o d -> p (o d)"),
                                      ALU.add).then_inc(job_free[jn % 2], 1)

            def rows_of(par, turn):
                for k in range(DT):
                    jn = J_EXPERT + par * DT + k
                    job_filled(dve, jn, turn * DT)
                    dve.tensor_copy(xeT[par][:, k, :], ps_t[jn % 2][:, 0:CAP]).then_inc(job_free[jn % 2], 1)

            def expert_hidden(par, turn):
                for ht in range(HT):
                    hidden(ehid[par][:, ht, :], ht, NCHUNK * HT + turn * (2 * HT) + par * HT + ht, CAP)

            rows_of(0, 0)
            with dve.Fori(0, E // 2 - 1) as i:
                expert_hidden(0, i)
                rows_of(1, i)
                expert_hidden(1, i)
                rows_of(0, i + 1)
            expert_hidden(0, E // 2 - 1)
            rows_of(1, E // 2 - 1)
            expert_hidden(1, E // 2 - 1)

        @block.scalar
        def _(act):
            act.sem_inc(ysb_ready, 2)
            act.wait_ge(consts, 2)

            def root(n, lo, cnt, rows=P):
                act.wait_ge(var_ready, n)
                act.activation(std[0:rows, lo:lo + cnt], mv[0:rows, lo:lo + cnt, 1], ACT.Sqrt, bias=eps[0:rows, :])\
                   .then_inc(std_ready, 1)

            n = 0
            for b in range(B):
                for _ in range(2):
                    n += 1
                    root(n, b * QT_N, QT_N)
            n += 1
            root(n, NT, B, CT)
            act.wait_ge(small_in, 16 * 8)
            act.activation(sq_junk[0:GE, :], cen[:, :], ACT.Square, accum_out=cstat[:, 0:1]).then_inc(act_seq, 1)
            act.wait_ge(act_seq, 1)
            act.activation(cstat[:, 1:2], cstat[:, 0:1], ACT.Sqrt).then_inc(std_ready, 1)

            act.preload_act_table(ACT.Exp)
            with act.Fori(0, HP) as hp:
                more = hp * (JOBS_HP // 2)
                for b in range(B):
                    j0 = JOBS_A + b * JOBS_B
                    n0 = hp * (B * UNITS) + b * UNITS

                    def exp(u):
                        act.wait_ge(rowmax, n0 + u + 1)
                        act.activation(probs[:, u % 2, :], ps_s[:, ROW0[u % 2]:ROW0[u % 2] + KEYS], ACT.Exp,
                                       bias=negmax[:, u % 2:u % 2 + 1],
                                       accum_out=rowsum[:, (u // 2) % 2, u % 2:u % 2 + 1]).then_inc(exp_done, 1)

                    def out_of(i, dst, src, scale=1.0):
                        job_filled(act, j0 + i, more)
                        act.activation(dst, src, ACT.Copy, scale=scale).then_inc(job_free[(j0 + i) % 2], 1)

                    bank = [ps_t[(j0 + i) % 2] for i in range(8)]
                    out_of(1, KTb[b][:, 512:1024], bank[1][:, :])
                    out_of(3, QTb[b][:, 0:512], bank[3][:, :], DH ** -0.5)
                    out_of(5, Vb[b][:, 0:4, :].rearrange("p k n -> p (k n)"), bank[5][:, :])
                    exp(0)
                    out_of(7, Vb[b][0:CT, 8, :], bank[7][0:CT, 0:P])
                    for u in range(UNITS):
                        i = 8 + u * 3
                        out_of(i, probsT[:, u % 2, 0:4, :].rearrange("p k n -> p (k n)"), ps_t[(j0 + i) % 2][:, :])
                        if u + 1 < UNITS:
                            exp(u + 1)
                        out_of(i + 2, probsT[0:CT, u % 2, 8, :], ps_t[(j0 + i + 2) % 2][0:CT, 0:P])

            jj = J_WOUT
            for t in range(NT):
                job_filled(act, jj)
                act.activation(oT[:, t % 2, 0:4, :].rearrange("p k n -> p (k n)"), ps_t[jj % 2][:, :], ACT.Copy)\
                   .then_inc(job_free[jj % 2], 1)
                jj += 2
            for g in range(NT // 4):
                root(n + g + 1, g * 4, 4)
            for g in range(NT // 4):
                act.wait_ge(h_ready, g + 1)
                for t in range(g * 4, g * 4 + 4):
                    ins = act.activation(sq_junk[:, :], h_sb[:, t, :], ACT.Square, accum_out=ssq[:, t:t + 1])
                    ins.then_inc(act_seq, 1)
                    act.wait_ge(act_seq, 1 + t + 1)
                jn = jj + g * DT + 1
                job_filled(act, jn)
                act.activation(hT[:, 1, g * 512:(g + 1) * 512], ps_t[jn % 2][:, :], ACT.Copy)\
                   .then_inc(job_free[jn % 2], 1)
            act.activation(rnorm[:, :], ssq[:, :], ACT.Sqrt).then_inc(norm_ready, 1)
            act.wait_ge(gate_in, 1)
            act.activation(posk[:, :, :], keep[:, :, :], ACT.Exp).then_inc(gate_exp, 1)

            act.preload_act_table(ACT.Silu)

            def silu_of(n, g, width):
                act.wait_ge(gu_ready, g + 1)
                act.activation(silu[n % 2][:, 0:width], ps_s[:, (n % 2) * 512:(n % 2) * 512 + width], ACT.Silu)\
                   .then_inc(silu_done, 1)

            with act.Fori(0, NCHUNK) as c:
                for ht in range(HT):
                    silu_of(ht, c * HT + ht, 512)

            ey_bank = (ps_o, ps_s[:, 2 * 512:3 * 512])

            def expert(par, turn):
                for ht in range(HT):
                    silu_of(ht, NCHUNK * HT + turn * (2 * HT) + par * HT + ht, CAP)
                y0 = turn * (2 * CTL) + par * CTL
                act.wait_ge(ids_in[par], turn * 32 + 32)
                for c, (_, rows) in enumerate(CAP_TILES):
                    act.wait_ge(ey_ready, y0 + 2 * CTL + c + 1)
                    act.activation(y_sb[par][0:rows, c, :], ey_bank[(par * CTL + c) % 2][0:rows, 0:D], ACT.Copy,
                                   scale=ids_s[0:rows, par, c, 1:2].bitcast(F32))\
                       .then_inc(ysb_ready, 1)

            with act.Fori(0, E // 2) as i:
                expert(0, i)
                expert(1, i)


_INS = ['x', 'ctx_1024', 'L0_xattn_ln_m_g', 'L0_xattn_ln_m_b', 'L0_xattn_ln_l_g', 'L0_xattn_ln_l_b', 'L0_xattn_Wq',
        'L0_xattn_Wkv', 'L0_xattn_Wout', 'L0_ffn_group_centroids', 'L0_ffn_expert_centroids', 'L0_ffn_bias',
        'L0_ffn_wg', 'L0_ffn_wu', 'L0_ffn_wd', 'L0_ffn_sg', 'L0_ffn_su', 'L0_ffn_sd']


def kernel(**inputs):
    import numpy as _np
    import concourse.bacc as _bacc
    from concourse import mybir as _mybir
    from concourse.bass_utils import run_bass_kernel_spmd as _run

    nc = _bacc.Bacc("TRN2", target_bir_lowering=False, num_devices=1)
    arrays, args = {}, []
    for name in _INS:
        a = _np.ascontiguousarray(inputs[name])
        arrays[f"in_{name}_dram"] = a
        args.append(nc.dram_tensor(f"in_{name}_dram", a.shape, _mybir.dt.from_np(a.dtype), kind="ExternalInput").ap())
    out = nc.dram_tensor("out_0_dram", inputs['x'].shape, F32, kind="ExternalOutput").ap()
    xattn_moe(nc, *args, out)
    r = _run(nc, [arrays], core_ids=[0])
    return r.results[0]["out_0_dram"]
```

```python
from contextlib import ExitStack

import concourse.bass as bass
from concourse import mybir

F32 = mybir.dt.float32
F32R = mybir.dt.float32r
I32 = mybir.dt.int32
U32 = mybir.dt.uint32
ALU = mybir.AluOpType
ACT = mybir.ActivationFunctionType
AX = mybir.AxisListType
P = 128


class Chain:

    def __init__(self, eng, sem):
        self.eng, self.sem, self.n = eng, sem, 0

    def done(self, ins):
        self.n += 1
        ins.then_inc(self.sem, 1)

    def wait(self):
        self.eng.wait_ge(self.sem, self.n)


QUADS = 4
KEY_TILES = 9
PROJECT = [("k", 0), ("k", 1), ("q", 0), ("q", 1), ("k", 2)]


def attention_plan():
    last = 2 * QUADS - 1

    def batch(b, before):
        def old(*ev):
            return ev, int(b == 0)

        def maximum(q, n):
            return ("max", q, n), 0

        q0 = b * QUADS
        av = [old("av", before, part) for part in range(KEY_TILES)]
        k0, k1, q_0, q_1, k2 = [((kind, b, i), 0) for kind, i in PROJECT]
        v0, v1, v2 = [(("v", b, i), 0) for i in range(3)]
        events = [k0, av[0], k1, av[1], q_0, av[2], q_1, av[3], k2, av[4], maximum(q0, 0), v0, maximum(q0, 1),
                  v1, maximum(q0, 2), v2, maximum(q0, 3), av[5], av[6], (("row", q0), 0), av[7]]
        for q in range(q0, q0 + QUADS):
            at = {q0: (0, 3, 5, 7), q0 + 1: (0, 4, 5, 7)}.get(q, (0, 2, 4, 6))
            for kt in range(KEY_TILES):
                events.append((("st", q, kt), 0))
                if q + 1 < q0 + QUADS and kt in at:
                    events.append(maximum(q + 1, at.index(kt)))
                if (q, kt) == (q0 + 1, 0):
                    events.append(old("norm", before))
                if (q, kt) == (q0 + 3, 0):
                    events.append((("norm", q - 2), 0))
                if q == q0 + 1 and kt in (5, 7):
                    events.append(old("out", before, kt // 2 - 2))
                if q == q0 + 3 and kt in (5, 7):
                    events.append((("out", q - 2, kt // 2 - 2), 0))
                if q > q0 and kt > 0:
                    events.append((("av", q - 1, kt - 1), 0))
                if (q, kt) == (7, 6):
                    events.append((("w", 0), -1))
            if q == q0:
                events.append(av[8])
            if q + 1 < q0 + QUADS:
                events.append((("row", q + 1), 0))
            if q > q0:
                events.append((("av", q - 1, KEY_TILES - 1), 0))
        return events

    pair = batch(0, last) + batch(1, QUADS - 1)
    first = [(("w", 0), 0)] + [(("cen", ev[2]), 0) if back == 1 else (ev, back) for ev, back in pair
                               if back < 1 or ev[0] == "out"]
    end = [(("av", last, part), 0) for part in range(KEY_TILES)]
    end += [(("norm", last), 0), (("out", last, 0), 0), (("out", last, 1), 0)]
    return first, pair, end, [ev for ev, back in pair if ev[0] in ("k", "q", "v", "row", "out")]


def xattn_moe(nc, x, ctx_in, ln_m_g, ln_m_b, ln_l_g, ln_l_b, Wq, Wkv, Wout, group_c, expert_c, e_bias,
              wg, wu, wd, sg, su, sd, out):
    B, S, D = x.shape
    CT = ctx_in.shape[1]
    INNER = Wq.shape[1]
    DH = 64
    H = INNER // DH
    HP = H // 2
    DT = D // P
    QT_N = S // P
    NT = B * QT_N
    NTOK = B * S
    KEYS = S + CT
    KT_N = QT_N + 1
    G, E = group_c.shape[0], expert_c.shape[0]
    TOPG, TOPK = G // 2, 4
    PER_G = E // G
    HID = wg.shape[2]
    HT = HID // P
    CAP = max(1, int(NTOK / E * TOPK * 1.25))
    CTL = -(-CAP // P)
    CROWS = -(-CAP // CTL)
    CAP_TILES = [(c, min(CROWS, CAP - c)) for c in range(0, CAP, CROWS)]
    SLOTS = E * CAP
    ROWS = NTOK + CAP
    EPS = 1e-5
    GE = G + E

    JOBS_A = B * DT * 2 + DT
    FIRST, PAIR, END, RING = attention_plan()
    JOBS_HP = len(RING)
    J_HT = JOBS_A + HP * JOBS_HP + 2
    assert DT == 2 and KT_N == KEY_TILES
    J_SHARED = J_HT + NT // 4 * DT
    J_EXPERT = J_SHARED + NT
    assert JOBS_A % 2 == JOBS_HP % 2 == J_SHARED % 2 == J_EXPERT % 2 == 0
    NCHUNK = NTOK // 512
    HI_HP = 10
    WPIECES = 4

    tbl = nc.dram_tensor("slot_table", [SLOTS + NTOK * TOPK, 2], I32, kind="Internal").ap()
    hrows = nc.dram_tensor("h_rows", [ROWS, D], F32, kind="Internal").ap()
    acc = nc.dram_tensor("acc_rows", [ROWS, D], F32, kind="Internal").ap()

    with ExitStack() as stack:
        def sb(name, shape, dt=F32):
            return stack.enter_context(nc.sbuf_tensor(name, shape, dt))

        def sem(name):
            return stack.enter_context(nc.semaphore(name))

        x_sb = sb("x_sb", [P, NT, D])
        ctx_sb = sb("ctx_sb", [CT, B, D])
        kvT = sb("kvT", [P, DT, B * KEYS])
        wout_sb = sb("wout_sb", [P, HP, D])
        ident4 = sb("ident4", [P, 4, P], F32R)
        mask4 = sb("mask4", [P, 4, P])

        W = DT * HID
        R_KV, R_REST = 2 * DT * B * KEYS, 6 * W + 2 * HT * 512
        arena_r = sb("arena_r", [P, R_KV + R_REST], F32R)
        arena = sb("arena", [P, max(6 * W + 4 * CTL * D + 4 * D + 4 * 512, 2 * KT_N * (512 + B * P) + DT * 3 * P + 2 * 512)])

        def carver(mem, start=0):
            at = [start]

            def carve(words, pattern=None, **dims):
                at[0] += words
                part = mem[:, at[0] - words:at[0]]
                return part.rearrange(pattern, **dims) if pattern else part
            return carve

        carve = carver(arena_r)
        kvT_hi, kvT_lo = (carve(DT * B * KEYS, "p (k n) -> p k n", k=DT) for _ in range(2))
        k1, k2 = ([carve(KEYS + 1) for _ in range(2)] for _ in range(2))
        q1, q2 = ([carve(S) for _ in range(2)] for _ in range(2))
        w_hi, w_lo = (carve(DT * 2 * P, "p (k c n) -> p k c n", k=DT, c=2) for _ in range(2))
        neg = [carve(P) for _ in range(2)]
        carve = carver(arena)
        probsT = carve(2 * KT_N * 512, "p (a k n) -> p a k n", a=2, k=KT_N)
        vals = carve(B * KT_N * 2 * P, "p (b k h n) -> p b k h n", b=B, k=KT_N, h=2)
        w_hp = carve(DT * 3 * P, "p (k c n) -> p k c n", k=DT, c=3)
        oT, rinv = (carve(512) for _ in range(2))

        carve = carver(arena_r)
        ws_hi, ws_lo = [None, carve(3 * W)], [None, carve(3 * W)]
        xe_hi, xe_lo = (carve(DT * CAP, "p (k n) -> p k n", k=DT) for _ in range(2))
        carve = carver(arena_r, R_KV)
        ws_hi[0], ws_lo[0] = carve(3 * W), carve(3 * W)
        hid_hi, hid_lo = (carve(HT * 512, "p (k n) -> p k n", k=HT) for _ in range(2))
        carve = carver(arena)
        w_raw = [carve(3 * W) for _ in range(2)]
        xg, y_sb = ([carve(CTL * D, "p (c n) -> p c n", c=CTL) for _ in range(2)] for _ in range(2))
        sacc = carve(4 * D, "p (t n) -> p t n", t=4)
        silu, hid32 = ([carve(512) for _ in range(2)] for _ in range(2))
        hT, hT_hi, hT_lo = kvT[:, :, 0:NTOK], kvT_hi[:, :, 0:NTOK], kvT_lo[:, :, 0:NTOK]

        def gate_up(w, i):
            return w[:, i * W:(i + 1) * W].rearrange("p (k n) -> p k n", k=DT)

        def down_of(w):
            return w[:, 2 * W:3 * W].rearrange("p (k n) -> p k n", k=HT)

        carve = carver(arena, 6 * W)
        z_sb = carve(NT * D, "p (t d) -> p t d", t=NT)
        h_sb = z_sb
        zc_sb = arena[0:CT, 0:B * D].rearrange("p (t d) -> p t d", t=B)
        flat_kv = kvT[:, :, :].rearrange("p k n -> p (k n)")
        onehot, picked = (flat_kv[:, i * NT * TOPK * E:(i + 1) * NT * TOPK * E]
                          .rearrange("p (t k e) -> p t k e", t=NT, k=TOPK) for i in range(2))

        ident = sb("ident", [P, P])
        lower = sb("lower", [P, P])
        ones = sb("ones", [P, P])
        zeros = sb("zeros", [P, ROWS * D // P - NTOK * D // P])
        tinit = sb("tinit", [E, CAP, 2], I32)
        gb = sb("gb", [P, 4, DT])
        eps = sb("eps", [P, 1])
        bias_bc = sb("bias_bc", [P, E])
        cen = sb("cen", [GE, D])
        cstat = sb("cstat", [GE, 4])
        cT = sb("cT", [P, DT, GE])
        stats = sb("stats", [P, NT, 6])
        mv = sb("mv", [P, NT + B, 2])
        cstats = sb("cstats", [CT, B, 6])
        std = sb("std", [P, NT + B])
        rstd = sb("rstd", [P, NT + B])
        ssq = sb("ssq", [P, NT])
        rnorm = sb("rnorm", [P, NT])
        sq_junk = sb("sq_junk", [P, D])
        sc = sb("sc", [P, NT, GE])
        masked = sb("masked", [P, NT, E])
        top8 = sb("top8", [P, NT, 8])
        top8i = sb("top8i", [P, NT, 8], U32)
        topf = sb("topf", [P, NT, TOPK])
        gmask = sb("gmask", [P, NT, G])
        chosen = sb("chosen", [P, NT, E])
        before = sb("before", [P, NT, E])
        posk = sb("posk", [P, NT, TOPK])
        keep = sb("keep", [P, NT, TOPK])
        dropslot = sb("dropslot", [P, NT, TOPK])
        slot = sb("slot", [P, NT, TOPK], I32)
        entry = sb("entry", [P, NT, TOPK, 2], I32)
        gsum = sb("gsum", [P, NT])
        iota_e = sb("iota_e", [P, E])

        ROWK = [slice(0, DH), slice(DH, P)]
        OTHER = [slice(DH, P), slice(0, DH)]
        MROW = [slice(DH, DH + 4), slice(0, 4)]
        K2ROWS = [DH + 4, P]
        ids_g = sb("ids_g", [P, 2, CTL, 2], I32)
        ids_s = sb("ids_s", [P, 2, CTL, 2], I32)

        ps_m = stack.enter_context(nc.psum_tensor("ps_m", [P, 3, 512], F32))
        ps_st = stack.enter_context(nc.psum_tensor("ps_st", [P, 2, 512], F32))
        ps_o = stack.enter_context(nc.psum_tensor("ps_o", [P, 512], F32))
        ps_t = [stack.enter_context(nc.psum_tensor(f"ps_t{i}", [P, 512], F32)) for i in range(2)]
        scores_m = ps_m[:, :, :].rearrange("p a n -> p (a n)")
        ey_bank = (ps_o, ps_m[:, 2, :])

        x_in = sem("x_in")
        small_in = sem("small_in")
        wout_in = sem("wout_in")
        w_in = sem("w_in")
        consts = sem("consts")
        pair_consts = sem("pair_consts")
        ones_ready = sem("ones_ready")
        dve_seq = sem("dve_seq")
        act_seq = sem("act_seq")
        pool_seq = sem("pool_seq")
        pool_step = sem("pool_step")
        var_ready = sem("var_ready")
        std_ready = sem("std_ready")
        z_ready = sem("z_ready")
        job_ready = [sem(f"job_ready{i}") for i in range(2)]
        job_free = [sem(f"job_free{i}") for i in range(2)]
        kv_ready = sem("kv_ready")
        kv_hi = sem("kv_hi")
        kv_split = sem("kv_split")
        pair_hi = sem("pair_hi")
        w_split = sem("w_split")
        w_hi_ready = sem("w_hi_ready")
        copies_in = [sem(f"copies_in{i}") for i in range(B)]
        max_ready = sem("max_ready")
        max_done = sem("max_done")
        st_ready = sem("st_ready")
        exp_done = sem("exp_done")
        o_ready = sem("o_ready")
        o_free = sem("o_free")
        rinv_ready = sem("rinv_ready")
        o_normed = sem("o_normed")
        x1_ready = sem("x1_ready")
        h_ready = sem("h_ready")
        hrows_out = sem("hrows_out")
        init_out = sem("init_out")
        norm_ready = sem("norm_ready")
        router_ready = sem("router_ready")
        chosen_ready = sem("chosen_ready")
        pos_ready = sem("pos_ready")
        gate_in = sem("gate_in")
        gate_exp = sem("gate_exp")
        slots_ready = sem("slots_ready")
        tbl_out = sem("tbl_out")
        h_hi = sem("h_hi")
        w_hi_done = sem("w_hi_done")
        w_lo_done = sem("w_lo_done")
        hid_ready = sem("hid_ready")
        hid_hi_done = sem("hid_hi_done")
        hid_done = sem("hid_done")
        xe_hi_done = sem("xe_hi_done")
        gu_ready = sem("gu_ready")
        silu_done = sem("silu_done")
        gu_free = sem("gu_free")
        sacc_out = [sem(f"sacc_out{i}") for i in range(2)]
        ew_in = [sem(f"ew_in{i}") for i in range(2)]
        idg_in = [sem(f"idg_in{i}") for i in range(2)]
        ids_in = [sem(f"ids_in{i}") for i in range(2)]
        rows_in = [sem(f"rows_in{i}") for i in range(2)]
        ey_ready = sem("ey_ready")
        ysb_ready = sem("ysb_ready")
        ysb_free = sem("ysb_free")
        add_out = sem("add_out")
        final_out = sem("final_out")

        def job_of(ev, end=False):
            if ev[0] == "cen":
                ev = ("out", 2 * QUADS - 1, ev[1])
            return JOBS_A + (ev[2] if end else RING.index(ev))

        def bank_free(eng, j, more=0):
            eng.wait_ge(job_free[j % 2], j // 2 + 1 + more)

        def job_done(eng, j, more=0):
            eng.wait_ge(job_free[j % 2], j // 2 + 2 + more)

        def job_filled(eng, j, more=0):
            eng.wait_ge(job_ready[j % 2], j // 2 + 1 + more)

        block = stack.enter_context(nc.Block())

        @block.sync
        def _(sp):
            for b in range(B):
                sp.dma_start(x_sb[:, b * QT_N:(b + 1) * QT_N, :],
                             x[b].rearrange("(t p) d -> p t d", p=P)).then_inc(x_in, 16)
            sp.dma_start(ctx_sb[:, :, :], ctx_in.rearrange("b t d -> t b d")).then_inc(small_in, 16)
            for i, v in enumerate((ln_l_g, ln_l_b, ln_m_g, ln_m_b)):
                sp.dma_start(gb[:, i, :], v.rearrange("(k p) -> p k", p=P), allow_slow_non_contiguous=True).then_inc(small_in, 16)
            sp.dma_start(bias_bc[:, :], e_bias.partition_broadcast(P)).then_inc(small_in, 16)
            sp.dma_start(cen[0:G, :], group_c).then_inc(small_in, 16)
            sp.dma_start(cen[G:GE, :], expert_c).then_inc(small_in, 16)
            sp.dma_start(wout_sb[:, :, :], Wout.rearrange("(h p) n -> p h n", p=P)).then_inc(wout_in, 16)
            sp.wait_ge(consts, 2)
            for t in (hrows, acc):
                sp.dma_start(t[NTOK:ROWS, :].rearrange("r d -> (r d)").rearrange("(p n) -> p n", p=P),
                             zeros[:, :]).then_inc(init_out, 16)
            sp.dma_start(tbl[0:SLOTS, :].rearrange("(e c) w -> e (c w)", e=E),
                         tinit[:, :, :].rearrange("e c w -> e (c w)")).then_inc(init_out, 16)

            def load_pair(hp):
                for i, (w, col) in enumerate(((Wq, 0), (Wkv, 0), (Wkv, INNER))):
                    sp.dma_start(w_hp[:, :, i, :],
                                 w[:, bass.ds(hp * P + col, P)].rearrange("(k p) n -> p k n", p=P))\
                      .then_inc(w_in, 16)

            load_pair(0)

            with sp.Fori(0, HP - 1) as hp:
                job_filled(sp, job_of(("v", B - 1, 2)), hp * (JOBS_HP // 2))
                load_pair(hp + 1)

            job_filled(sp, job_of(("v", B - 1, 2)), (HP - 1) * (JOBS_HP // 2))
            sp.sem_inc(w_in, 48)

            def load_weights(slot, gate, up, down):
                for i, w in enumerate((gate, up, down)):
                    sp.dma_start(w_raw[slot][:, i * W:(i + 1) * W].rearrange("p (k n) -> p k n", n=w.shape[-1]),
                                 w).then_inc(ew_in[slot], 16)

            def of_expert(w, e):
                return w[bass.ds(e, 1)].rearrange("o (k p) n -> p (o k) n", p=P)

            job_done(sp, J_HT - 2)
            job_done(sp, J_HT - 1)
            load_weights(0, *(w.rearrange("(k p) n -> p k n", p=P) for w in (sg, su, sd)))
            load_weights(1, *(of_expert(w, 0) for w in (wg, wu, wd)))
            for g in range(NT // 4):
                sp.wait_ge(h_ready, g + 1)
                sp.dma_start(hrows[g * 4 * P:(g + 1) * 4 * P, :].rearrange("(t p) d -> p t d", p=P),
                             h_sb[:, g * 4:(g + 1) * 4, :]).then_inc(hrows_out, 16)
            with sp.Fori(0, NCHUNK) as c:
                for half in range(2):
                    for i in range(2):
                        job_done(sp, J_SHARED + half * 2 + i, c * 2)
                    sp.dma_start(acc[bass.ds(c * 512 + half * 256, 256), :].rearrange("(t p) d -> p t d", p=P),
                                 sacc[:, half * 2:half * 2 + 2, :]).then_inc(sacc_out[half], 16)
            sp.wait_ge(tbl_out, 16 * NT * TOPK)

            def load_ids(dst, e, done):
                sp.dma_start(dst[0:CROWS, 0:CTL - 1, :],
                             tbl[bass.ds(e * CAP, (CTL - 1) * CROWS), :].rearrange("(c p) w -> p c w", p=CROWS))\
                  .then_inc(done, 16)
                lo, rows = CAP_TILES[-1]
                sp.dma_start(dst[0:rows, CTL - 1, :], tbl[bass.ds(e * CAP + lo, rows), :]).then_inc(done, 16)

            def feed(par, turn, weights):
                e = turn * 2 + par
                sp.wait_ge(job_ready[1], (J_EXPERT // 2 - 2 + 1) + e)
                load_ids(ids_g[:, par], e, idg_in[par])
                if weights:
                    sp.wait_ge(w_lo_done, e * WPIECES)
                    load_weights((par + 1) % 2, *(of_expert(w, e) for w in (wg, wu, wd)))
                sp.wait_ge(ysb_free, e + 1)
                load_ids(ids_s[:, par], e, ids_in[par])

            feed(0, 0, False)
            feed(1, 0, True)
            with sp.Fori(1, E // 2) as i:
                feed(0, i, True)
                feed(1, i, True)
            sp.wait_ge(add_out, 16 * CTL * E)
            sp.dma_start(out.rearrange("b s d -> (b s) d"), acc[0:NTOK, :]).then_inc(final_out, 16)
            sp.wait_ge(final_out, 16)

        @block.gpsimd
        def _(pool):
            seq = Chain(pool, pool_seq)
            seq.done(pool.memset(zeros[:, :], 0.0))
            seq.done(pool.memset(tinit[:, :, :].bitcast(F32), 0.0))
            seq.done(pool.memset(ident[:, :], 0.0))
            seq.done(pool.memset(lower[:, :], 1.0))
            seq.done(pool.memset(ones[:, :], 1.0))
            seq.done(pool.memset(eps[:, :], EPS))
            seq.wait()
            seq.done(pool.iota(tinit[:, :, 0], pattern=[[1, CAP]], base=NTOK, channel_multiplier=0))
            seq.done(pool.affine_select(out=ident[:, :], in_=ident[:, :], compare_op=ALU.not_equal, fill=1.0,
                                        base=0, pattern=[[-1, P]], channel_multiplier=1))
            seq.done(pool.affine_select(out=lower[:, :], in_=lower[:, :], compare_op=ALU.is_gt, fill=0.0,
                                        base=0, pattern=[[1, P]], channel_multiplier=-1))
            seq.done(pool.iota(iota_e[:, :], pattern=[[1, E]], base=0, channel_multiplier=0,
                               allow_small_or_imprecise_dtypes=True))
            seq.done(pool.iota(dropslot[:, :, :], pattern=[[P * TOPK, NT], [1, TOPK]], base=SLOTS,
                               channel_multiplier=TOPK, allow_small_or_imprecise_dtypes=True))
            for k in range(TOPK):
                seq.done(pool.iota(entry[:, :, k, 0], pattern=[[P, NT]], base=0, channel_multiplier=1))
            seq.wait()
            pool.sem_inc(consts, 2)
            seq.done(pool.memset(mask4[:, :, :], 0.0))
            seq.wait()
            for base in (0, -DH):
                seq.done(pool.affine_select(out=mask4[:, :, :], in_=mask4[:, :, :], compare_op=ALU.not_equal,
                                            fill=1.0, base=base, pattern=[[-1, 4], [0, P]], channel_multiplier=1))
                seq.wait()
            for part, value in [
                    (part.bitcast(F32), value) for h in range(2)
                    for part, value in ((neg[h], 0.0), (k1[h][:, KEYS:KEYS + 1], 0.0), (k2[h][OTHER[h], :], 0.0),
                                        (q2[h][OTHER[h], :], 0.0), (k2[h][MROW[h], :], 1.0))]:
                seq.done(pool.memset(part, value))
                seq.wait()
            pool.sem_inc(pair_consts, 1)
            pool.sem_inc(ysb_free, 2)

            def attend(events, pair, end=False):
                for ev, back in events:
                    hp = pair - back
                    if ev[0] == "k" and ev[2] == 2:
                        b = ev[1]
                        pool.wait_ge(pair_hi, hp * HI_HP + (b + 1) * 5)
                        pool.sem_inc(pool_step, 1)
                        for h in range(2):
                            pool.dma_start(k2[h][ROWK[h], 0:KEYS], k1[h][ROWK[h], 0:KEYS])\
                                .then_inc(copies_in[b], 16)
                            pool.dma_start(q1[h][OTHER[h], :], q1[h][ROWK[h], :]).then_inc(copies_in[b], 16)
                    if ev[0] == "norm":
                        pool.wait_ge(rinv_ready, hp * 4 + ev[1] // 2 + 1)
                        pool.tensor_tensor(oT[:, :], oT[:, :], rinv[:, :], ALU.mult).then_inc(o_normed, 1)

            attend(FIRST, 0)
            with pool.Fori(1, HP) as hp:
                attend(PAIR, hp)
            attend(END, HP - 1, end=True)

            pool.wait_ge(init_out, 48)
            pool.wait_ge(slots_ready, 1)
            for t in range(NT):
                for k in range(TOPK):
                    pool.indirect_dma_start(
                        out=tbl[:, :], out_offset=bass.IndirectOffsetOnAxis(ap=slot[:, t, k:k + 1].bitcast(U32), axis=0),
                        in_=entry[:, t, k, :], in_offset=None).then_inc(tbl_out, 16)

            def gather(par, turn):
                pool.wait_ge(hrows_out, 16 * (NT // 4))
                pool.wait_ge(idg_in[par], turn * 32 + 32)
                pool.sem_inc(pool_step, 1)
                for c, (_, rows) in enumerate(CAP_TILES):
                    pool.indirect_dma_start(
                        out=xg[par][0:rows, c, :], out_offset=None, in_=hrows[:, :],
                        in_offset=bass.IndirectOffsetOnAxis(ap=ids_g[0:rows, par, c, 0:1].bitcast(U32), axis=0))\
                        .then_inc(rows_in[par], 16)

            def add(par, turn):
                e = turn * 2 + par
                pool.wait_ge(sacc_out[0], 16 * NCHUNK + 16)
                pool.wait_ge(sacc_out[1], 16 * NCHUNK + 16)
                pool.wait_ge(ysb_ready, e * CTL + CTL + 2)
                pool.sem_inc(pool_step, 1)
                for c, (_, rows) in enumerate(CAP_TILES):
                    pool.indirect_dma_start(
                        out=acc[:, :], in_=y_sb[par][0:rows, c, :], in_offset=None, compute_op=ALU.add,
                        out_offset=bass.IndirectOffsetOnAxis(ap=ids_s[0:rows, par, c, 0:1].bitcast(U32), axis=0))\
                        .then_inc(add_out, 16)
                pool.wait_ge(add_out, (e + 1) * 16 * CTL)
                pool.sem_inc(ysb_free, 1)

            gather(0, 0)
            gather(1, 0)
            with pool.Fori(0, E // 2 - 1) as i:
                gather(0, i + 1)
                add(0, i)
                gather(1, i + 1)
                add(1, i)
            add(0, E // 2 - 1)
            add(1, E // 2 - 1)

        @block.tensor
        def _(pe):
            pe.wait_ge(consts, 2)
            j = 0
            for b in range(B):
                pe.wait_ge(z_ready, b + 1)
                for k in range(DT):
                    for half in range(2):
                        bank_free(pe, j)
                        for i in range(4):
                            mm = pe.transpose(ps_t[j % 2][:, i * P:(i + 1) * P],
                                              z_sb[:, b * QT_N + half * 4 + i, k * P:(k + 1) * P], ident[:, :])
                        mm.then_inc(job_ready[j % 2], 1)
                        j += 1
            pe.wait_ge(z_ready, B + 1)
            for k in range(DT):
                bank_free(pe, j)
                for b in range(B):
                    mm = pe.transpose(ps_t[j % 2][:, b * P:b * P + CT], zc_sb[:, b, k * P:(k + 1) * P],
                                      ident[0:CT, 0:CT])
                mm.then_inc(job_ready[j % 2], 1)
                j += 1
            assert j == JOBS_A
            job_done(pe, j - 2)
            job_done(pe, j - 1)

            def product(ps, pairs):
                for n, (a, m) in enumerate(pairs):
                    mm = pe.matmul(ps, a, m, start=(n == 0), stop=(n == len(pairs) - 1))
                return mm

            def split_pairs(a_hi, a_lo, m_hi, m_lo):
                return [(a_hi, m_hi), (a_hi, m_lo), (a_lo, m_hi)]

            pe.wait_ge(kv_split, B * DT)
            pe.wait_ge(pair_consts, 1)
            pe.wait_ge(ones_ready, 1)
            pe.wait_ge(wout_in, 16)

            def attend(events, pair, end=False):
                for ev, back in events:
                    kind, a = ev[0], ev[1]
                    hp = pair - back
                    more = (pair + end) * (JOBS_HP // 2)
                    if kind == "cen" or ev in RING:
                        jn = job_of(ev, end)
                        bank = ps_t[jn % 2]
                        bank_free(pe, jn, more)
                    if kind in "kq":
                        if ev == ("k", 0, 0):
                            pe.wait_ge(w_split, hp + 1)
                        lo, w = ((0, 512), (512, 512), (S, CT))[ev[2]]
                        lo += a * KEYS
                        c = int(kind == "k")
                        if w == CT:
                            pairs = [(w_hp[:, k, c, :], kvT[:, k, lo:lo + w]) for k in range(DT)]
                        else:
                            pairs = [p for k in range(DT)
                                     for p in split_pairs(w_hi[:, k, c, :], w_lo[:, k, c, :],
                                                          kvT_hi[:, k, lo:lo + w], kvT_lo[:, k, lo:lo + w])]
                        product(bank[:, 0:w], pairs).then_inc(job_ready[jn % 2], 1)
                    if kind == "v":
                        for s_, t in enumerate(((0, 1, 2, 3), (4, 5, 6, 7), (8,))[ev[2]]):
                            rows = P if t < QT_N else CT
                            lo = a * KEYS + t * P
                            mm = product(bank[0:rows, s_ * P:(s_ + 1) * P],
                                         [(kvT[:, k, lo:lo + rows], w_hp[:, k, 2, :]) for k in range(DT)])
                        mm.then_inc(job_ready[jn % 2], 1)
                    if kind == "max":
                        b, h, half = a // QUADS, a % 2, a % QUADS // 2
                        if a % QUADS == 0 and ev[2] == 0:
                            pe.wait_ge(pair_hi, hp * HI_HP + b * 5 + 5)
                        pe.wait_ge(max_done, hp * (8 * 4) + a * 4 + ev[2] + 1)
                        c = half * 512 + ev[2] * P
                        for lo, w in ((0, 512), (512, 512), (S, CT + 1)):
                            mm = pe.matmul(scores_m[:, lo:lo + w], q1[h][ROWK[h], c:c + P],
                                           k1[h][ROWK[h], lo:lo + w], start=True, stop=True)
                        mm.then_inc(max_ready, 1)
                    if kind == "row":
                        pe.wait_ge(max_done, hp * (8 * 4) + a * 4 + 4 + 1)
                        pe.matmul(bank[:, :], neg[a % 2], ident4[:, :, :].rearrange("p a n -> p (a n)"),
                                  start=True, stop=True).then_inc(job_ready[jn % 2], 1)
                    if kind == "st":
                        b, h, c, kt = a // QUADS, a % 2, a % QUADS // 2 * 512, ev[2]
                        n = a * KT_N + kt
                        rows = P if kt < QT_N else CT
                        r = slice(kt * P, kt * P + rows)
                        kr = slice(0, K2ROWS[h])
                        if kt == 0 and a % QUADS == 0:
                            pe.wait_ge(copies_in[b], hp * 64 + 64)
                            job_done(pe, job_of(("k", b, 1)), more)
                            job_done(pe, job_of(("k", b, 2)), more)
                        pe.wait_ge(exp_done, hp * 72 + n + 1)
                        pe.matmul(ps_st[0:rows, n % 2, :], k1[h][:, r], q1[h][:, c:c + 512],
                                  start=True, stop=False)
                        if kt == 0:
                            job_done(pe, job_of(("row", a)), more)
                        pe.matmul(ps_st[0:rows, n % 2, :], k2[h][kr, r], q2[h][kr, c:c + 512],
                                  start=False, stop=True).then_inc(st_ready, 1)
                    if kind == "av":
                        kt = ev[2]
                        if kt == 0:
                            pe.wait_ge(o_free, hp * 8 + a + 1)
                            job_done(pe, job_of(("v", a // QUADS, 1)), hp * (JOBS_HP // 2))
                            job_done(pe, job_of(("v", a // QUADS, 2)), hp * (JOBS_HP // 2))
                        pe.wait_ge(exp_done, hp * 72 + a * KT_N + kt + 1 + 2)
                        rows = P if kt < QT_N else CT
                        mm = pe.matmul(ps_o[:, :], vals[0:rows, a // QUADS, kt, a % 2, :], probsT[0:rows, a % 2, kt, :],
                                       start=(kt == 0), stop=(kt == KT_N - 1))
                        if kt == KT_N - 1:
                            mm.then_inc(o_ready, 1)
                    if kind == "cen":
                        pe.wait_ge(z_ready, B + 2)
                        pe.transpose(bank[:, 0:GE], cen[:, a * P:(a + 1) * P], ident[0:GE, 0:GE])\
                          .then_inc(job_ready[jn % 2], 1)
                    if kind == "out":
                        pe.wait_ge(o_normed, hp * 4 + a // 2 + 1)
                        for i in range(2):
                            c = (ev[2] * 2 + i) * P
                            mm = pe.matmul(bank[:, i * D:(i + 1) * D], oT[:, c:c + P],
                                           wout_sb[:, bass.ds(hp, 1), :].rearrange("p o n -> p (o n)"),
                                           start=True, stop=True)
                        mm.then_inc(job_ready[jn % 2], 1)

            pe.wait_ge(w_in, 48)
            attend(FIRST, 0)
            with pe.Fori(1, HP) as hp:
                attend(PAIR, hp)
            attend(END, HP - 1, end=True)

            j = J_HT

            def turn_h(g):
                nonlocal j
                pe.wait_ge(h_ready, g + 1)
                for k in range(DT):
                    bank_free(pe, j)
                    for i in range(4):
                        mm = pe.transpose(ps_t[j % 2][:, i * P:(i + 1) * P],
                                          h_sb[:, g * 4 + i, k * P:(k + 1) * P], ident[:, :])
                    mm.then_inc(job_ready[j % 2], 1)
                    j += 1

            def score(g):
                for k in range(DT):
                    job_done(pe, J_HT + g * DT + k)
                for t in range(g * 4, g * 4 + 4):
                    lo = (t % 8) * GE
                    for k in range(DT):
                        mm = pe.matmul(router_bank[t // 8][:, lo:lo + GE], hT[:, k, t * P:(t + 1) * P],
                                       cT[:, k, :], start=(k == 0), stop=(k == DT - 1))
                mm.then_inc(router_ready, 1)

            router_bank = (ps_m[:, 2, :], ps_o)
            for g in range(NT // 4):
                turn_h(g)
                if g:
                    score(g - 1)
            assert j == J_SHARED
            score(NT // 4 - 1)
            pe.wait_ge(chosen_ready, 1)
            pe.matmul(ps_o[:, :], lower[:, :], chosen[:, :, :].rearrange("p t e -> p (t e)"), start=True, stop=False)
            pe.matmul(ps_o[:, :], ones[:, :], before[:, :, :].rearrange("p t e -> p (t e)"), start=False, stop=True)\
              .then_inc(pos_ready, 1)

            def up(slot, width, x_hi, x_lo, g0):
                for ht in range(HT):
                    pe.wait_ge(gu_free, g0 + ht + 1)
                    c = slice(ht * P, (ht + 1) * P)
                    for i, bank in enumerate((ps_m, ps_st)):
                        w_h, w_l = gate_up(ws_hi[slot], i), gate_up(ws_lo[slot], i)
                        mm = product(bank[:, ht % 2, 0:width],
                                     [p for k in range(DT)
                                      for p in split_pairs(w_h[:, k, c], w_l[:, k, c], x_hi(k), x_lo(k))])
                    mm.then_inc(gu_ready, 1)

            def down(slot, tiles, banks, g0, claim, done):
                d_h, d_l = down_of(ws_hi[slot]), down_of(ws_lo[slot])
                begun = (0, 1)
                order = [(k, c) for c in begun for k in range(HT - 1)] + [(HT - 1, c) for c in begun]
                order += [(k, c) for c in range(2, len(tiles)) for k in range(HT)]
                for k, c in order:
                    lo, rows = tiles[c]
                    if k == 0:
                        claim(c)
                    if c == 0:
                        pe.wait_ge(hid_done, g0 + k + 1 + 2)
                    for n, (a, m) in enumerate(split_pairs(hid_hi[:, k, lo:lo + rows], hid_lo[:, k, lo:lo + rows],
                                                           d_h[:, k, :], d_l[:, k, :])):
                        mm = pe.matmul(banks[c], a, m, start=(k == 0 and n == 0), stop=(k == HT - 1 and n == 2))
                    if k == HT - 1:
                        mm.then_inc(done[c], 1)

            pe.wait_ge(w_lo_done, WPIECES)
            with pe.Fori(0, NCHUNK) as c:
                up(0, 512, lambda k: hT_hi[:, k, bass.ds(c * 512, 512)],
                   lambda k: hT_lo[:, k, bass.ds(c * 512, 512)], c * HT)
                down(0, [(i * P, P) for i in range(4)], [ps_t[i % 2][:, 0:D] for i in range(4)], c * HT,
                     lambda i: bank_free(pe, J_SHARED + i, c * 2), [job_ready[i % 2] for i in range(4)])

            def turn_rows(par, turn):
                pe.wait_ge(rows_in[par], turn * (16 * CTL) + 16 * CTL)
                for k in range(DT):
                    jj = J_EXPERT + par * DT + k
                    bank_free(pe, jj, turn * DT)
                    for c, (lo, rows) in enumerate(CAP_TILES):
                        mm = pe.transpose(ps_t[jj % 2][:, lo:lo + rows], xg[par][0:rows, c, k * P:(k + 1) * P],
                                          ident[0:rows, 0:rows])
                    mm.then_inc(job_ready[jj % 2], 1)

            def expert_up(par, turn):
                e = turn * 2 + par
                pe.wait_ge(w_lo_done, e * WPIECES + 2 * WPIECES)
                for k in range(DT):
                    job_done(pe, J_EXPERT + par * DT + k, turn * DT)
                up((par + 1) % 2, CAP, lambda k: xe_hi[:, k, :], lambda k: xe_lo[:, k, :],
                   NCHUNK * HT + turn * (2 * HT) + par * HT)

            def expert_down(par, turn):
                y0 = turn * (2 * CTL) + par * CTL
                down((par + 1) % 2, CAP_TILES,
                     [ey_bank[(par * CTL + c) % 2][0:rows, 0:D] for c, (_, rows) in enumerate(CAP_TILES)],
                     NCHUNK * HT + turn * (2 * HT) + par * HT,
                     lambda c: pe.wait_ge(ysb_ready, y0 + c + 1), [ey_ready] * CTL)

            turn_rows(0, 0)
            with pe.Fori(0, E // 2 - 1) as i:
                expert_up(0, i)
                turn_rows(1, i)
                expert_down(0, i)
                expert_up(1, i)
                turn_rows(0, i + 1)
                expert_down(1, i)
            last = E // 2 - 1
            expert_up(0, last)
            turn_rows(1, last)
            expert_down(0, last)
            expert_up(1, last)
            expert_down(1, last)

        @block.vector
        def _(dve):
            seq = Chain(dve, dve_seq)
            for s in job_free:
                dve.sem_inc(s, 1)
            dve.sem_inc(o_free, 1)
            dve.sem_inc(max_done, 1)
            dve.sem_inc(gu_free, 2)
            dve.sem_inc(hid_done, 2)
            for s in sacc_out:
                dve.sem_inc(s, 16)

            def spread(src, sts, lo, n, rows=P):
                for t in range(n):
                    seq.done(dve.bn_stats(sts[0:rows, t, :], src[0:rows, t, :]))
                seq.wait()
                for t in range(n):
                    ins = dve.bn_aggr(mv[0:rows, lo + t, :], sts[0:rows, t, :])
                    seq.done(ins)
                seq.wait()

            def normed(dst, src, lo, n, rows=P):
                seq.done(dve.reciprocal(rstd[0:rows, lo:lo + n], std[0:rows, lo:lo + n]))
                seq.wait()
                scaled(dst, src, lo, n, rows)

            def scaled(dst, src, lo, n, rows=P):
                for t in range(n):
                    seq.done(dve.tensor_scalar(dst[0:rows, t, :], src[0:rows, t, :], mv[0:rows, lo + t, 0:1],
                                               rstd[0:rows, lo + t:lo + t + 1], ALU.subtract, ALU.mult))
                seq.wait()

            dve.wait_ge(x_in, 16 * B)
            tiles = [slice(b * QT_N, (b + 1) * QT_N) for b in range(B)]
            for b in range(B):
                spread(x_sb[:, tiles[b], :], stats, b * QT_N, QT_N)
                dve.sem_inc(var_ready, 1)
            for b in range(B):
                t = tiles[b]
                dve.wait_ge(std_ready, b + 1)
                seq.done(dve.reciprocal(rstd[:, t], std[:, t]))
                seq.wait()
                for _ in range(2):
                    seq.done(dve.tensor_tensor(mv[:, t, 1], mv[:, t, 1], rstd[:, t], ALU.mult))
                    seq.wait()
                dve.sem_inc(var_ready, 1)
            for b in range(B):
                t = tiles[b]
                dve.wait_ge(std_ready, B + b + 1)
                seq.done(dve.reciprocal(std[:, t], std[:, t]))
                seq.wait()
                seq.done(dve.tensor_tensor(rstd[:, t], rstd[:, t], std[:, t], ALU.mult))
                seq.wait()
                scaled(z_sb[:, t, :], x_sb[:, t, :], b * QT_N, QT_N)
                dve.sem_inc(z_ready, 1)
            nv = 2 * B
            dve.wait_ge(small_in, 16 * 8)
            for b in range(B):
                for k in range(DT):
                    jj = b * DT * 2 + k * 2
                    job_filled(dve, jj)
                    dve.tensor_scalar(kvT[:, k, b * KEYS:b * KEYS + 512], ps_t[jj % 2][:, :], gb[:, 0, k:k + 1],
                                      gb[:, 1, k:k + 1], ALU.mult, ALU.add).then_inc(job_free[jj % 2], 1)
            spread(ctx_sb, cstats, NT, B, CT)
            dve.sem_inc(var_ready, 1)
            nv += 1
            dve.wait_ge(std_ready, nv)
            normed(zc_sb, ctx_sb, NT, B, CT)
            dve.sem_inc(z_ready, 1)
            for k in range(DT):
                jj = B * DT * 2 + k
                job_filled(dve, jj)
                dve.tensor_scalar(kvT[:, k, :].rearrange("p (b n) -> p b n", b=B)[:, :, S:KEYS],
                                  ps_t[jj % 2][:, 0:B * P].rearrange("p (b n) -> p b n", b=B)[:, :, 0:CT],
                                  gb[:, 2, k:k + 1], gb[:, 3, k:k + 1], ALU.mult, ALU.add)\
                   .then_inc(job_free[jj % 2], 1)
            job_done(dve, B * DT * 2 + DT - 2)
            job_done(dve, B * DT * 2 + DT - 1)
            dve.sem_inc(kv_ready, 1)
            for k in range(DT):
                for b in range(B):
                    c = slice(b * KEYS, (b + 1) * KEYS)
                    dve.wait_ge(kv_hi, k * B + b + 1)
                    dve.tensor_tensor(kvT_lo[:, k, c], kvT[:, k, c], kvT_hi[:, k, c].bitcast(F32), ALU.subtract)\
                       .then_inc(kv_split, 1)
            dve.wait_ge(std_ready, nv + 1)
            seq.done(dve.tensor_scalar(cstat[:, 2:3], cstat[:, 1:2], 1e-12, None, ALU.max))
            seq.wait()
            seq.done(dve.reciprocal(cstat[:, 3:4], cstat[:, 2:3]))
            seq.wait()
            seq.done(dve.tensor_scalar(cen[:, :], cen[:, :], cstat[:, 3:4], None, ALU.mult))
            seq.wait()
            dve.sem_inc(z_ready, 1)

            dve.wait_ge(pair_consts, 1)
            seq.done(dve.tensor_copy(ident4[:, :, :], ident[:, :].unsqueeze(1).broadcast_to([P, 4, P])))
            seq.done(dve.memset(vals[:, :, :, :, :], 1.0))
            seq.wait()
            dve.sem_inc(ones_ready, 1)

            def attend(events, pair, end=False):
                for ev, back in events:
                    kind, a = ev[0], ev[1]
                    hp = pair - back
                    more = (pair + end) * (JOBS_HP // 2)
                    if kind == "cen" or ev in RING:
                        jn = job_of(ev, end)
                        bank, free = ps_t[jn % 2], job_free[jn % 2]
                    if kind == "w":
                        dve.wait_ge(w_hi_ready, hp + 1)
                        dve.tensor_tensor(w_lo[:, :, :, :], w_hp[:, :, 0:2, :], w_hi[:, :, :, :].bitcast(F32),
                                          ALU.subtract).then_inc(w_split, 1)
                    if kind in "kq":
                        lo, w = ((0, 512), (512, 512), (S, CT))[ev[2]]
                        dve.wait_ge(pair_hi, hp * HI_HP + a * 5 + PROJECT.index((kind, ev[2])) + 1)
                        for h in range(2):
                            if kind == "k":
                                ins = dve.tensor_tensor(k1[h][OTHER[h], lo:lo + w], bank[ROWK[h], 0:w],
                                                        k1[h][ROWK[h], lo:lo + w].bitcast(F32), ALU.subtract)
                            else:
                                ins = dve.scalar_tensor_tensor(q2[h][ROWK[h], lo:lo + w], bank[ROWK[h], 0:w],
                                                               DH ** -0.5, q1[h][ROWK[h], lo:lo + w].bitcast(F32),
                                                               ALU.mult, ALU.subtract)
                        ins.then_inc(free, 1)
                    if kind == "max":
                        dve.wait_ge(max_ready, hp * 32 + a * 4 + ev[2] + 1)
                        c = MROW[a % 2].start + ev[2]
                        dve.tensor_reduce(neg[a % 2][:, c:c + 1], scores_m[:, 0:KEYS], AX.X, ALU.max, negate=True)\
                           .then_inc(max_done, 1)
                    if kind == "row":
                        r = MROW[a % 2]
                        c = a % QUADS // 2 * 512
                        job_filled(dve, jn, more)
                        dve.tensor_tensor(q2[a % 2][r, c:c + 512], bank[r, :],
                                          mask4[r, :, :].rearrange("p a n -> p (a n)"), ALU.mult).then_inc(free, 1)
                    if kind == "norm":
                        dve.wait_ge(o_free, hp * 8 + a + 2)
                        dve.reciprocal(rinv[:, :], rinv[:, :]).then_inc(rinv_ready, 1)
                    if kind == "cen":
                        job_filled(dve, jn, more)
                        dve.tensor_copy(cT[:, a, :], bank[:, 0:GE]).then_inc(free, 1)
                    if kind == "out":
                        t = a // QUADS * QT_N + a % QUADS // 2 * 4 + ev[2] * 2
                        job_filled(dve, jn, more)
                        dve.tensor_tensor(x_sb[:, t:t + 2, :], x_sb[:, t:t + 2, :],
                                          bank[:, :].rearrange("p (t n) -> p t n", t=2), ALU.add).then_inc(free, 1)

            attend(FIRST, 0)
            with dve.Fori(1, HP) as hp:
                attend(PAIR, hp)
            attend(END, HP - 1, end=True)

            def weights_lo(slot, idx, piece):
                c = slice(piece * 3 * W // WPIECES, (piece + 1) * 3 * W // WPIECES)
                dve.wait_ge(w_hi_done, idx + 1)
                dve.tensor_tensor(ws_lo[slot][:, c], w_raw[slot][:, c], ws_hi[slot][:, c].bitcast(F32),
                                  ALU.subtract).then_inc(w_lo_done, 1)

            job_done(dve, J_HT - 2)
            job_done(dve, J_HT - 1)
            jj = J_HT
            for g in range(NT // 4):
                lo = g * 4
                spread(x_sb[:, lo:lo + 4, :], stats[:, lo:lo + 4, :], lo, 4)
                dve.sem_inc(var_ready, 1)
            for g in range(NT // 4):
                lo = g * 4
                dve.wait_ge(std_ready, nv + 1 + g + 1)
                normed(h_sb[:, lo:lo + 4, :], x_sb[:, lo:lo + 4, :], lo, 4)
                dve.sem_inc(h_ready, 1)
            for g in range(NT // 4):
                for k in range(DT):
                    c = slice(g * 512, (g + 1) * 512)
                    dve.wait_ge(h_hi, g * DT + k + 1)
                    dve.tensor_copy(hT[:, k, c], ps_t[jj % 2][:, :])
                    dve.tensor_tensor(hT_lo[:, k, c], ps_t[jj % 2][:, :], hT_hi[:, k, c].bitcast(F32), ALU.subtract)\
                       .then_inc(job_free[jj % 2], 1)
                    jj += 1
            for piece in range(WPIECES):
                weights_lo(0, piece, piece)
            dve.wait_ge(norm_ready, 1)
            seq.done(dve.tensor_scalar(rnorm[:, :], rnorm[:, :], 1e-12, None, ALU.max))
            seq.wait()
            seq.done(dve.reciprocal(ssq[:, :], rnorm[:, :]))
            seq.wait()
            dve.wait_ge(router_ready, NT // 4)
            for half, bank in enumerate((ps_m[:, 2, 0:8 * GE], ps_o[:, 0:8 * GE])):
                seq.done(dve.tensor_tensor(sc[:, half * 8:half * 8 + 8, :],
                                           bank.rearrange("p (t g) -> p t g", t=8),
                                           ssq[:, half * 8:half * 8 + 8].unsqueeze(2).broadcast_to([P, 8, GE]),
                                           ALU.mult))
            seq.wait()

            def top4(src, width):
                for t in range(NT):
                    seq.done(dve.max(top8[:, t, :], src[:, t, 0:width]))
                seq.wait()
                for t in range(NT):
                    seq.done(dve.max_index(top8i[:, t, :], top8[:, t, :], src[:, t, 0:width]))
                seq.wait()
                seq.done(dve.tensor_copy(topf[:, :, :], top8i[:, :, 0:TOPK]))
                seq.wait()

            def hot(dst, width):
                seq.done(dve.tensor_tensor(dst, topf[:, :, :].unsqueeze(3).broadcast_to([P, NT, TOPK, width]),
                                           iota_e[:, 0:width].unsqueeze(1).unsqueeze(1)
                                           .broadcast_to([P, NT, TOPK, width]), ALU.is_equal))
                seq.wait()

            dve.wait_ge(consts, 2)
            top4(sc, G)
            gh = picked[:, :, :, 0:G]
            hot(gh, G)
            seq.done(dve.tensor_reduce(gmask[:, :, :], gh.rearrange("p t k g -> p t g k"), AX.X, ALU.add))
            seq.done(dve.tensor_tensor(sc[:, :, G:GE], sc[:, :, G:GE],
                                       bias_bc[:, :].unsqueeze(1).broadcast_to([P, NT, E]), ALU.add))
            seq.wait()
            m4 = masked[:, :, :].rearrange("p t (g i) -> p t g i", i=PER_G)
            seq.done(dve.tensor_tensor(m4, sc[:, :, G:GE].rearrange("p t (g i) -> p t g i", i=PER_G),
                                       gmask[:, :, :].unsqueeze(3).broadcast_to([P, NT, G, PER_G]), ALU.mult))
            seq.wait()
            seq.done(dve.tensor_scalar(gmask[:, :, :], gmask[:, :, :], -1.0, 1e9, ALU.add, ALU.mult))
            seq.wait()
            seq.done(dve.tensor_tensor(m4, m4, gmask[:, :, :].unsqueeze(3).broadcast_to([P, NT, G, PER_G]), ALU.add))
            seq.wait()
            top4(masked, E)
            seq.done(dve.tensor_tensor(keep[:, :, :], top8[:, :, 0:TOPK], top8[:, :, 0:1].broadcast_to([P, NT, TOPK]),
                                       ALU.subtract))
            seq.wait()
            dve.sem_inc(gate_in, 1)
            hot(onehot[:, :, :, :], E)
            seq.done(dve.tensor_reduce(chosen[:, :, :], onehot[:, :, :, :].rearrange("p t k e -> p t e k"),
                                       AX.X, ALU.add))
            seq.done(dve.memset(before[:, 0, :], 0.0))
            seq.wait()
            for t in range(1, NT):
                seq.done(dve.tensor_tensor(before[:, t, :], before[:, t - 1, :], chosen[:, t - 1, :], ALU.add))
                seq.wait()
            dve.sem_inc(chosen_ready, 1)
            dve.wait_ge(gate_exp, 1)
            seq.done(dve.tensor_reduce(gsum[:, :], posk[:, :, :], AX.X, ALU.add))
            seq.wait()
            seq.done(dve.reciprocal(gsum[:, :], gsum[:, :]))
            seq.wait()
            seq.done(dve.tensor_tensor(entry[:, :, :, 1].bitcast(F32), posk[:, :, :],
                                       gsum[:, :].unsqueeze(2).broadcast_to([P, NT, TOPK]), ALU.mult))
            seq.wait()
            dve.wait_ge(pos_ready, 1)
            seq.done(dve.tensor_tensor(picked[:, :, :, :], onehot[:, :, :, :],
                                       ps_o[:, :].rearrange("p (t e) -> p t e", t=NT).unsqueeze(2)
                                       .broadcast_to([P, NT, TOPK, E]), ALU.mult))
            seq.wait()
            seq.done(dve.tensor_reduce(posk[:, :, :], picked[:, :, :, :], AX.X, ALU.add))
            seq.wait()
            seq.done(dve.tensor_scalar(keep[:, :, :], posk[:, :, :], float(CAP), None, ALU.is_lt))
            seq.done(dve.tensor_scalar(topf[:, :, :], topf[:, :, :], float(CAP), None, ALU.mult))
            seq.wait()
            seq.done(dve.tensor_tensor(posk[:, :, :], posk[:, :, :], topf[:, :, :], ALU.add))
            seq.wait()
            seq.done(dve.tensor_tensor(posk[:, :, :], posk[:, :, :], dropslot[:, :, :], ALU.subtract))
            seq.wait()
            seq.done(dve.tensor_tensor(posk[:, :, :], posk[:, :, :], keep[:, :, :], ALU.mult))
            seq.wait()
            seq.done(dve.tensor_tensor(slot[:, :, :], posk[:, :, :], dropslot[:, :, :], ALU.add))
            seq.wait()
            dve.sem_inc(slots_ready, 1)

            def hidden(g0, width, between=None):
                def low(ht):
                    dve.wait_ge(hid_hi_done, g0 + ht + 1)
                    dve.tensor_tensor(hid_lo[:, ht, 0:width], hid32[ht % 2][:, 0:width],
                                      hid_hi[:, ht, 0:width].bitcast(F32), ALU.subtract).then_inc(hid_done, 1)

                for ht in range(HT):
                    dve.wait_ge(hid_done, g0 + ht + 1)
                    dve.wait_ge(silu_done, g0 + ht + 1)
                    dve.tensor_tensor(hid32[ht % 2][:, 0:width], silu[ht % 2][:, 0:width],
                                      ps_st[:, ht % 2, 0:width], ALU.mult).then_inc(gu_free, 1)
                    if ht:
                        low(ht - 1)
                    if between:
                        between(ht)
                low(HT - 1)

            dve.wait_ge(hrows_out, 16 * (NT // 4))
            with dve.Fori(0, NCHUNK) as c:
                hidden(c * HT, 512)
                for i in range(4):
                    jn = J_SHARED + i
                    job_filled(dve, jn, c * 2)
                    if i % 2 == 0:
                        dve.wait_ge(sacc_out[i // 2], c * 16 + 16)
                    dve.tensor_tensor(sacc[:, i, :], ps_t[jn % 2][:, 0:D],
                                      x_sb[:, bass.ds(c * 4 + i, 1), :].rearrange("p o d -> p (o d)"),
                                      ALU.add).then_inc(job_free[jn % 2], 1)

            def rows_lo(par, turn):
                for k in range(DT):
                    jn = J_EXPERT + par * DT + k
                    dve.wait_ge(xe_hi_done, turn * (2 * DT) + par * DT + k + 1)
                    dve.tensor_tensor(xe_lo[:, k, :], ps_t[jn % 2][:, 0:CAP], xe_hi[:, k, :].bitcast(F32),
                                      ALU.subtract).then_inc(job_free[jn % 2], 1)

            def expert(par, turn, more=True):
                n = turn * (2 * WPIECES) + (par + 2) * WPIECES
                hidden(NCHUNK * HT + turn * (2 * HT) + par * HT, CAP,
                       (lambda ht: ht < 2 and weights_lo(par, n + ht, ht)) if more else None)
                if more:
                    rows_lo((par + 1) % 2, turn + par)
                    for piece in range(2, WPIECES):
                        weights_lo(par, n + piece, piece)

            for piece in range(WPIECES):
                weights_lo(1, WPIECES + piece, piece)
            rows_lo(0, 0)
            with dve.Fori(0, E // 2 - 1) as i:
                expert(0, i)
                expert(1, i)
            expert(0, E // 2 - 1)
            expert(1, E // 2 - 1, False)

        @block.scalar
        def _(act):
            act.sem_inc(ysb_ready, 2)
            act.wait_ge(consts, 2)

            def root(n, lo, cnt, rows=P):
                act.wait_ge(var_ready, n)
                act.activation(std[0:rows, lo:lo + cnt], mv[0:rows, lo:lo + cnt, 1], ACT.Sqrt, bias=eps[0:rows, :])\
                   .then_inc(std_ready, 1)

            roots = 2 * B + 1
            for i in range(2):
                for b in range(B):
                    root(i * B + b + 1, b * QT_N, QT_N)
            act.wait_ge(small_in, 16 * 8)
            for b in range(B):
                for k in range(DT):
                    jn = b * DT * 2 + k * 2 + 1
                    job_filled(act, jn)
                    act.activation(kvT[:, k, b * KEYS + 512:b * KEYS + S], ps_t[jn % 2][:, :], ACT.Identity,
                                   scale=gb[:, 0, k:k + 1], bias=gb[:, 1, k:k + 1]).then_inc(job_free[jn % 2], 1)
            root(roots, NT, B, CT)
            for k in range(DT):
                job_done(act, B * DT * 2 + k)
            act.activation(sq_junk[0:GE, :], cen[:, :], ACT.Square, accum_out=cstat[:, 0:1]).then_inc(act_seq, 1)
            act.wait_ge(act_seq, 1)
            act.activation(cstat[:, 1:2], cstat[:, 0:1], ACT.Sqrt).then_inc(std_ready, 1)

            act.wait_ge(kv_ready, 1)
            for k in range(DT):
                for b in range(B):
                    c = slice(b * KEYS, (b + 1) * KEYS)
                    act.activation(kvT_hi[:, k, c], kvT[:, k, c], ACT.Copy).then_inc(kv_hi, 1)
            act.preload_act_table(ACT.Exp)
            act.sem_inc(exp_done, 2)

            def attend(events, pair, end=False):
                for ev, back in events:
                    kind, a = ev[0], ev[1]
                    hp = pair - back
                    more = (pair + end) * (JOBS_HP // 2)
                    if kind == "w":
                        act.wait_ge(w_in, hp * 48 + 48)
                        act.activation(w_hi[:, :, :, :], w_hp[:, :, 0:2, :], ACT.Copy).then_inc(w_hi_ready, 1)
                    if kind in "kq":
                        jn = job_of(ev, end)
                        lo, w = ((0, 512), (512, 512), (S, CT))[ev[2]]
                        job_filled(act, jn, more)
                        for h in range(2):
                            ins = act.activation((k1 if kind == "k" else q1)[h][ROWK[h], lo:lo + w],
                                                 ps_t[jn % 2][ROWK[h], 0:w],
                                                 ACT.Copy, scale=1.0 if kind == "k" else DH ** -0.5)
                        ins.then_inc(pair_hi, 1)
                    if kind == "v":
                        t, n = ((0, 4), (4, 4), (8, 1))[ev[2]]
                        rows = P if t < QT_N else CT
                        jn = job_of(ev, end)
                        job_filled(act, jn, more)
                        for h in range(2):
                            ins = act.activation(vals[0:rows, a, t:t + n, h, ROWK[h]],
                                                 ps_t[jn % 2][0:rows, 0:n * P]
                                                 .rearrange("p (t h d) -> p h t d", t=n, h=2)[:, h], ACT.Copy)
                        ins.then_inc(job_free[jn % 2], 1)
                    if kind == "av" and ev[2] == KT_N - 1:
                        own, sums = ROWK[a % 2], OTHER[a % 2]
                        act.wait_ge(o_ready, hp * 8 + a + 1)
                        act.activation(oT[own, :], ps_o[own, :], ACT.Copy)
                        act.activation(rinv[own, :], ps_o[sums, :], ACT.Copy).then_inc(o_free, 1)
                    if kind == "out" and ev[2] == 1:
                        job_filled(act, job_of(ev, end), more)
                    if kind == "st":
                        n = a * KT_N + ev[2]
                        rows = P if ev[2] < QT_N else CT
                        act.wait_ge(st_ready, hp * 72 + n + 1)
                        act.activation(probsT[0:rows, a % 2, ev[2], :], ps_st[0:rows, n % 2, :], ACT.Exp)\
                           .then_inc(exp_done, 1)

            attend(FIRST, 0)
            with act.Fori(1, HP) as hp:
                attend(PAIR, hp)
            attend(END, HP - 1, end=True)

            jj = J_HT
            for g in range(NT // 4):
                root(roots + g + 1, g * 4, 4)
            for g in range(NT // 4):
                act.wait_ge(h_ready, g + 1)
                for t in range(g * 4, g * 4 + 4):
                    ins = act.activation(sq_junk[:, :], h_sb[:, t, :], ACT.Square, accum_out=ssq[:, t:t + 1])
                    ins.then_inc(act_seq, 1)
                    act.wait_ge(act_seq, 1 + t + 1)
                for k in range(DT):
                    jn = jj + g * DT + k
                    job_filled(act, jn)
                    act.activation(hT_hi[:, k, g * 512:(g + 1) * 512], ps_t[jn % 2][:, :], ACT.Copy)\
                       .then_inc(h_hi, 1)

            def weights_hi(slot, piece):
                c = slice(piece * 3 * W // WPIECES, (piece + 1) * 3 * W // WPIECES)
                act.activation(ws_hi[slot][:, c], w_raw[slot][:, c], ACT.Copy).then_inc(w_hi_done, 1)

            act.wait_ge(ew_in[0], 48)
            for piece in range(WPIECES):
                weights_hi(0, piece)
            act.activation(rnorm[:, :], ssq[:, :], ACT.Sqrt).then_inc(norm_ready, 1)
            act.wait_ge(gate_in, 1)
            act.activation(posk[:, :, :], keep[:, :, :], ACT.Exp).then_inc(gate_exp, 1)

            act.preload_act_table(ACT.Silu)

            def activate(g0, width, between=None):
                def high(ht):
                    act.wait_ge(gu_free, g0 + ht + 2 + 1)
                    act.activation(hid_hi[:, ht, 0:width], hid32[ht % 2][:, 0:width], ACT.Copy)\
                       .then_inc(hid_hi_done, 1)

                for ht in range(HT):
                    act.wait_ge(gu_ready, g0 + ht + 1)
                    act.activation(silu[ht % 2][:, 0:width], ps_m[:, ht % 2, 0:width], ACT.Silu)\
                       .then_inc(silu_done, 1)
                    if ht:
                        high(ht - 1)
                    if between:
                        between(ht)
                high(HT - 1)

            with act.Fori(0, NCHUNK) as c:
                activate(c * HT, 512)

            def rows_hi(par, turn):
                for k in range(DT):
                    jn = J_EXPERT + par * DT + k
                    job_filled(act, jn, turn * DT)
                    act.activation(xe_hi[:, k, :], ps_t[jn % 2][:, 0:CAP], ACT.Copy).then_inc(xe_hi_done, 1)

            def expert(par, turn, more=True):
                if more:
                    act.wait_ge(ew_in[par], turn * 48 + (96 if par == 0 else 96))
                activate(NCHUNK * HT + turn * (2 * HT) + par * HT, CAP,
                         (lambda ht: ht < 2 and weights_hi(par, ht)) if more else None)
                if more:
                    rows_hi((par + 1) % 2, turn + par)
                    for piece in range(2, WPIECES):
                        weights_hi(par, piece)
                y0 = turn * (2 * CTL) + par * CTL
                act.wait_ge(ids_in[par], turn * 32 + 32)
                for c, (_, rows) in enumerate(CAP_TILES):
                    act.wait_ge(ey_ready, y0 + c + 1)
                    act.activation(y_sb[par][0:rows, c, :], ey_bank[(par * CTL + c) % 2][0:rows, 0:D], ACT.Copy,
                                   scale=ids_s[0:rows, par, c, 1:2].bitcast(F32)).then_inc(ysb_ready, 1)

            act.wait_ge(hid_done, NCHUNK * HT + 2)
            act.wait_ge(job_ready[1], J_EXPERT // 2)
            act.wait_ge(ew_in[1], 48)
            for piece in range(WPIECES):
                weights_hi(1, piece)
            rows_hi(0, 0)
            with act.Fori(0, E // 2 - 1) as i:
                expert(0, i)
                expert(1, i)
            expert(0, E // 2 - 1)
            expert(1, E // 2 - 1, False)


_INS = ['x', 'ctx_1024', 'L0_xattn_ln_m_g', 'L0_xattn_ln_m_b', 'L0_xattn_ln_l_g', 'L0_xattn_ln_l_b', 'L0_xattn_Wq',
        'L0_xattn_Wkv', 'L0_xattn_Wout', 'L0_ffn_group_centroids', 'L0_ffn_expert_centroids', 'L0_ffn_bias',
        'L0_ffn_wg', 'L0_ffn_wu', 'L0_ffn_wd', 'L0_ffn_sg', 'L0_ffn_su', 'L0_ffn_sd']


def kernel(**inputs):
    import numpy as _np
    import concourse.bacc as _bacc
    from concourse import mybir as _mybir
    from concourse.bass_utils import run_bass_kernel_spmd as _run

    nc = _bacc.Bacc("TRN2", target_bir_lowering=False, num_devices=1)
    arrays, args = {}, []
    for name in _INS:
        a = _np.ascontiguousarray(inputs[name])
        arrays[f"in_{name}_dram"] = a
        args.append(nc.dram_tensor(f"in_{name}_dram", a.shape, _mybir.dt.from_np(a.dtype), kind="ExternalInput").ap())
    out = nc.dram_tensor("out_0_dram", inputs['x'].shape, F32, kind="ExternalOutput").ap()
    xattn_moe(nc, *args, out)
    r = _run(nc, [arrays], core_ids=[0])
    return r.results[0]["out_0_dram"]
```

```python
from contextlib import ExitStack

import concourse.bass as bass
from concourse import mybir

F32 = mybir.dt.float32
F32R = mybir.dt.float32r
I32 = mybir.dt.int32
U32 = mybir.dt.uint32
ALU = mybir.AluOpType
ACT = mybir.ActivationFunctionType
AX = mybir.AxisListType
P = 128


class Chain:

    def __init__(self, eng, sem):
        self.eng, self.sem, self.n = eng, sem, 0

    def done(self, ins):
        self.n += 1
        ins.then_inc(self.sem, 1)

    def wait(self):
        self.eng.wait_ge(self.sem, self.n)


QUADS = 4
KEY_TILES = 9
PROJECT = [("k", 0), ("k", 1), ("k", 2), ("q", 0), ("q", 1)]


def attention_plan():
    last = 2 * QUADS - 1

    def batch(b, before):
        def old(*ev):
            return ev, int(b == 0)

        def maximum(q, n):
            return ("max", q, n), 0

        q0 = b * QUADS
        av = [old("av", before, part) for part in range(KEY_TILES)]
        k0, k1, k2, q_0, q_1 = [((kind, b, i), 0) for kind, i in PROJECT]
        v0, v1, v2 = [(("v", b, i), 0) for i in range(3)]
        events = [k0, av[0], k1, av[1], k2, av[2], q_0, av[3], maximum(q0, 0), q_1, maximum(q0, 1), v0, av[4],
                  maximum(q0, 2), v1, maximum(q0, 3), v2, av[5], (("row", q0), 0), av[6]]
        for q in range(q0, q0 + QUADS):
            at = {q0: (0, 3, 5, 7), q0 + 1: (0, 4, 5, 7)}.get(q, (0, 2, 4, 6))
            for kt in range(KEY_TILES):
                events.append((("st", q, kt), 0))
                if (q, kt) == (q0, 4):
                    events.append(av[7])
                if q + 1 < q0 + QUADS and kt in at:
                    events.append(maximum(q + 1, at.index(kt)))
                if (q, kt) == (q0 + 1, 0):
                    events.append(old("norm", before))
                if (q, kt) == (q0 + 3, 0):
                    events.append((("norm", q - 2), 0))
                if q == q0 + 1 and kt in (5, 7):
                    events.append(old("out", before, kt // 2 - 2))
                if q == q0 + 3 and kt in (5, 7):
                    events.append((("out", q - 2, kt // 2 - 2), 0))
                if q > q0 and kt > 0:
                    events.append((("av", q - 1, kt - 1), 0))
                if (q, kt) == (7, 6):
                    events.append((("w", 0), -1))
            if q == q0:
                events.append(av[8])
            if q + 1 < q0 + QUADS:
                events.append((("row", q + 1), 0))
            if q > q0:
                events.append((("av", q - 1, KEY_TILES - 1), 0))
        return events

    pair = batch(0, last) + batch(1, QUADS - 1)
    first = [(("w", 0), 0)] + [(("cen", ev[2]), 0) if back == 1 else (ev, back) for ev, back in pair
                               if back < 1 or ev[0] == "out"]
    end = [(("av", last, part), 0) for part in range(KEY_TILES)]
    end += [(("norm", last), 0), (("out", last, 0), 0), (("out", last, 1), 0)]
    return first, pair, end, [ev for ev, back in pair if ev[0] in ("k", "q", "v", "row", "out")]


def xattn_moe(nc, x, ctx_in, ln_m_g, ln_m_b, ln_l_g, ln_l_b, Wq, Wkv, Wout, group_c, expert_c, e_bias,
              wg, wu, wd, sg, su, sd, out):
    B, S, D = x.shape
    CT = ctx_in.shape[1]
    INNER = Wq.shape[1]
    DH = 64
    H = INNER // DH
    HP = H // 2
    DT = D // P
    QT_N = S // P
    NT = B * QT_N
    NTOK = B * S
    KEYS = S + CT
    KT_N = QT_N + 1
    G, E = group_c.shape[0], expert_c.shape[0]
    TOPG, TOPK = G // 2, 4
    PER_G = E // G
    HID = wg.shape[2]
    HT = HID // P
    CAP = max(1, int(NTOK / E * TOPK * 1.25))
    CTL = -(-CAP // P)
    CROWS = -(-CAP // CTL)
    CAP_TILES = [(c, min(CROWS, CAP - c)) for c in range(0, CAP, CROWS)]
    SLOTS = E * CAP
    ROWS = NTOK + CAP
    EPS = 1e-5
    GE = G + E

    JOBS_A = B * DT * 2 + DT
    FIRST, PAIR, END, RING = attention_plan()
    JOBS_HP = len(RING)
    J_HT = JOBS_A + HP * JOBS_HP + 2
    assert DT == 2 and KT_N == KEY_TILES and TOPG == TOPK and B == 2
    J_SHARED = J_HT + NT // 4 * DT
    J_EXPERT = J_SHARED + NT
    assert JOBS_A % 2 == JOBS_HP % 2 == J_SHARED % 2 == J_EXPERT % 2 == 0
    NCHUNK = NTOK // 512
    HI_HP = B * len(PROJECT)
    O_HP = B * QUADS
    MAX_HP = O_HP * 4
    ST_HP = O_HP * KT_N
    WPIECES = 4

    tbl = nc.dram_tensor("slot_table", [SLOTS + NTOK * TOPK, 2], I32, kind="Internal").ap()
    hrows = nc.dram_tensor("h_rows", [ROWS, D], F32, kind="Internal").ap()
    acc = nc.dram_tensor("acc_rows", [ROWS, D], F32, kind="Internal").ap()

    with ExitStack() as stack:
        def sb(name, shape, dt=F32):
            return stack.enter_context(nc.sbuf_tensor(name, shape, dt))

        def sem(name):
            return stack.enter_context(nc.semaphore(name))

        x_sb = sb("x_sb", [P, NT, D])
        ctx_sb = sb("ctx_sb", [CT, B, D])
        kvT = sb("kvT", [P, DT, B * KEYS])
        wout_sb = sb("wout_sb", [P, HP, D])
        ident4 = sb("ident4", [P, 4, P], F32R)
        mask4 = sb("mask4", [P, 4, P])

        W = DT * HID
        R_KV, R_REST = 2 * DT * B * KEYS, 6 * W + 2 * HT * 512
        arena_r = sb("arena_r", [P, R_KV + R_REST], F32R)
        arena = sb("arena", [P, max(6 * W + 4 * CTL * D + 4 * D + 4 * 512,
                                    2 * KT_N * (512 + B * P) + DT * 3 * P + 2 * 512)])

        def carver(mem, start=0):
            at = [start]

            def carve(words, pattern=None, **dims):
                at[0] += words
                part = mem[:, at[0] - words:at[0]]
                return part.rearrange(pattern, **dims) if pattern else part
            return carve

        carve = carver(arena_r)
        kvT_hi, kvT_lo = (carve(DT * B * KEYS, "p (k n) -> p k n", k=DT) for _ in range(2))
        k1, k2 = ([carve(KEYS + 1) for _ in range(2)] for _ in range(2))
        q1, q2 = ([carve(S) for _ in range(2)] for _ in range(2))
        w_hi, w_lo = (carve(DT * 2 * P, "p (k c n) -> p k c n", k=DT, c=2) for _ in range(2))
        neg = [carve(P) for _ in range(2)]
        carve = carver(arena)
        probsT = carve(2 * KT_N * 512, "p (a k n) -> p a k n", a=2, k=KT_N)
        vals = carve(B * KT_N * 2 * P, "p (b k h n) -> p b k h n", b=B, k=KT_N, h=2)
        w_hp = carve(DT * 3 * P, "p (k c n) -> p k c n", k=DT, c=3)
        oT, rinv = (carve(512) for _ in range(2))

        carve = carver(arena_r)
        ws_hi, ws_lo = [None, carve(3 * W)], [None, carve(3 * W)]
        xe_hi, xe_lo = (carve(DT * CAP, "p (k n) -> p k n", k=DT) for _ in range(2))
        carve = carver(arena_r, R_KV)
        ws_hi[0], ws_lo[0] = carve(3 * W), carve(3 * W)
        hid_hi, hid_lo = (carve(HT * 512, "p (k n) -> p k n", k=HT) for _ in range(2))
        carve = carver(arena)
        w_raw = [carve(3 * W) for _ in range(2)]
        xg, y_sb = ([carve(CTL * D, "p (c n) -> p c n", c=CTL) for _ in range(2)] for _ in range(2))
        sacc = carve(4 * D, "p (t n) -> p t n", t=4)
        silu, hid32 = ([carve(512) for _ in range(2)] for _ in range(2))
        hT, hT_hi, hT_lo = kvT[:, :, 0:NTOK], kvT_hi[:, :, 0:NTOK], kvT_lo[:, :, 0:NTOK]

        def gate_up(w, i):
            return w[:, i * W:(i + 1) * W].rearrange("p (k n) -> p k n", k=DT)

        def down_of(w):
            return w[:, 2 * W:3 * W].rearrange("p (k n) -> p k n", k=HT)

        carve = carver(arena, 6 * W)
        z_sb = carve(NT * D, "p (t d) -> p t d", t=NT)
        h_sb = z_sb
        zc_sb = arena[0:CT, 0:B * D].rearrange("p (t d) -> p t d", t=B)
        flat_kv = kvT[:, :, :].rearrange("p k n -> p (k n)")
        onehot, picked = (flat_kv[:, i * NT * TOPK * E:(i + 1) * NT * TOPK * E]
                          .rearrange("p (t k e) -> p t k e", t=NT, k=TOPK) for i in range(2))

        ident = sb("ident", [P, P])
        lower = sb("lower", [P, P])
        ones = sb("ones", [P, P])
        zeros = sb("zeros", [P, ROWS * D // P - NTOK * D // P])
        tinit = sb("tinit", [E, CAP, 2], I32)
        gb = sb("gb", [P, 4, DT])
        eps = sb("eps", [P, 1])
        bias_bc = sb("bias_bc", [P, E])
        cen = sb("cen", [GE, D])
        cstat = sb("cstat", [GE, 4])
        cT = sb("cT", [P, DT, GE])
        stats = sb("stats", [P, NT, 6])
        mv = sb("mv", [P, NT + B, 2])
        cstats = sb("cstats", [CT, B, 6])
        std = sb("std", [P, NT + B])
        rstd = sb("rstd", [P, NT + B])
        ssq = sb("ssq", [P, NT])
        rnorm = sb("rnorm", [P, NT])
        sq_junk = sb("sq_junk", [P, D])
        sc = sb("sc", [P, NT, GE])
        masked = sb("masked", [P, NT, E])
        top8 = sb("top8", [P, NT, 8])
        top8i = sb("top8i", [P, NT, 8], U32)
        topf = sb("topf", [P, NT, TOPK])
        gmask = sb("gmask", [P, NT, G])
        chosen = sb("chosen", [P, NT, E])
        before = sb("before", [P, NT, E])
        posk = sb("posk", [P, NT, TOPK])
        keep = sb("keep", [P, NT, TOPK])
        dropslot = sb("dropslot", [P, NT, TOPK])
        slot = sb("slot", [P, NT, TOPK], I32)
        entry = sb("entry", [P, NT, TOPK, 2], I32)
        gsum = sb("gsum", [P, NT])
        iota_e = sb("iota_e", [P, E])

        ROWK = [slice(0, DH), slice(DH, P)]
        OTHER = [slice(DH, P), slice(0, DH)]
        MROW = [slice(DH, DH + 4), slice(0, 4)]
        K2ROWS = [DH + 4, P]
        ids_g = sb("ids_g", [P, 2, CTL, 2], I32)
        ids_s = sb("ids_s", [P, 2, CTL, 2], I32)

        ps_m = stack.enter_context(nc.psum_tensor("ps_m", [P, 3, 512], F32))
        ps_st = stack.enter_context(nc.psum_tensor("ps_st", [P, 2, 512], F32))
        ps_o = stack.enter_context(nc.psum_tensor("ps_o", [P, 512], F32))
        ps_t = [stack.enter_context(nc.psum_tensor(f"ps_t{i}", [P, 512], F32)) for i in range(2)]
        scores_m = ps_m[:, :, :].rearrange("p a n -> p (a n)")
        ey_bank = (ps_o, ps_m[:, 2, :])

        x_in, small_in, wout_in, w_in = (sem(n) for n in ("x_in", "small_in", "wout_in", "w_in"))
        init_out, hrows_out, tbl_out = (sem(n) for n in ("init_out", "hrows_out", "tbl_out"))
        add_out, final_out = sem("add_out"), sem("final_out")
        sacc_out = [sem(f"sacc_out{i}") for i in range(2)]
        ew_in = [sem(f"ew_in{i}") for i in range(2)]
        idg_in = [sem(f"idg_in{i}") for i in range(2)]
        ids_in = [sem(f"ids_in{i}") for i in range(2)]
        rows_in = [sem(f"rows_in{i}") for i in range(2)]
        copies_in = [sem(f"copies_in{i}") for i in range(B)]
        dve_seq, act_seq, pool_seq = (sem(n) for n in ("dve_seq", "act_seq", "pool_seq"))
        pool_step = sem("pool_step")
        consts, pair_consts, ones_ready = (sem(n) for n in ("consts", "pair_consts", "ones_ready"))
        job_ready = [sem(f"job_ready{i}") for i in range(2)]
        job_free = [sem(f"job_free{i}") for i in range(2)]
        var_ready, std_ready, z_ready = (sem(n) for n in ("var_ready", "std_ready", "z_ready"))
        kv_ready, kv_hi = sem("kv_ready"), sem("kv_hi")
        kv_split = [sem(f"kv_split{i}") for i in range(B)]
        w_hi_ready, w_split, pair_hi = (sem(n) for n in ("w_hi_ready", "w_split", "pair_hi"))
        max_ready, max_done = sem("max_ready"), sem("max_done")
        st_ready, exp_done = sem("st_ready"), sem("exp_done")
        o_ready, o_free, rinv_ready, o_normed = (sem(n) for n in ("o_ready", "o_free", "rinv_ready", "o_normed"))
        h_ready, h_hi, norm_ready, router_ready, chosen_ready, pos_ready, gate_in, gate_exp, slots_ready = (
            sem(n) for n in ("h_ready", "h_hi", "norm_ready", "router_ready", "chosen_ready", "pos_ready",
                             "gate_in", "gate_exp", "slots_ready"))
        w_hi_done, w_lo_done, xe_hi_done = (sem(n) for n in ("w_hi_done", "w_lo_done", "xe_hi_done"))
        gu_ready, silu_done, gu_free = (sem(n) for n in ("gu_ready", "silu_done", "gu_free"))
        hid_hi_done, hid_done = sem("hid_hi_done"), sem("hid_done")
        ey_ready, ysb_ready, ysb_free = (sem(n) for n in ("ey_ready", "ysb_ready", "ysb_free"))

        def job_of(ev, end=False):
            if ev[0] == "cen":
                ev = ("out", 2 * QUADS - 1, ev[1])
            return JOBS_A + (ev[2] if end else RING.index(ev))

        def bank_free(eng, j, more=0):
            eng.wait_ge(job_free[j % 2], j // 2 + 1 + more)

        def job_done(eng, j, more=0):
            eng.wait_ge(job_free[j % 2], j // 2 + 2 + more)

        def job_filled(eng, j, more=0):
            eng.wait_ge(job_ready[j % 2], j // 2 + 1 + more)

        block = stack.enter_context(nc.Block())

        @block.sync
        def _(sp):
            for b in range(B):
                sp.dma_start(x_sb[:, b * QT_N:(b + 1) * QT_N, :],
                             x[b].rearrange("(t p) d -> p t d", p=P)).then_inc(x_in, 16)
            sp.dma_start(ctx_sb[:, :, :], ctx_in.rearrange("b t d -> t b d")).then_inc(small_in, 16)
            for i, v in enumerate((ln_l_g, ln_l_b, ln_m_g, ln_m_b)):
                sp.dma_start(gb[:, i, :], v.rearrange("(k p) -> p k", p=P), allow_slow_non_contiguous=True)\
                  .then_inc(small_in, 16)
            sp.dma_start(bias_bc[:, :], e_bias.partition_broadcast(P)).then_inc(small_in, 16)
            sp.dma_start(cen[0:G, :], group_c).then_inc(small_in, 16)
            sp.dma_start(cen[G:GE, :], expert_c).then_inc(small_in, 16)
            sp.dma_start(wout_sb[:, :, :], Wout.rearrange("(h p) n -> p h n", p=P)).then_inc(wout_in, 16)
            sp.wait_ge(consts, 2)
            for t in (hrows, acc):
                sp.dma_start(t[NTOK:ROWS, :].rearrange("r d -> (r d)").rearrange("(p n) -> p n", p=P),
                             zeros[:, :]).then_inc(init_out, 16)
            sp.dma_start(tbl[0:SLOTS, :].rearrange("(e c) w -> e (c w)", e=E),
                         tinit[:, :, :].rearrange("e c w -> e (c w)")).then_inc(init_out, 16)

            def load_pair(hp):
                for i, (w, col) in enumerate(((Wq, 0), (Wkv, 0), (Wkv, INNER))):
                    sp.dma_start(w_hp[:, :, i, :],
                                 w[:, bass.ds(hp * P + col, P)].rearrange("(k p) n -> p k n", p=P))\
                      .then_inc(w_in, 16)

            load_pair(0)

            with sp.Fori(0, HP - 1) as hp:
                job_filled(sp, job_of(("v", B - 1, 2)), hp * (JOBS_HP // 2))
                load_pair(hp + 1)

            job_filled(sp, job_of(("v", B - 1, 2)), (HP - 1) * (JOBS_HP // 2))
            sp.sem_inc(w_in, 48)

            def load_weights(slot, gate, up, down):
                for i, w in enumerate((gate, up, down)):
                    sp.dma_start(w_raw[slot][:, i * W:(i + 1) * W].rearrange("p (k n) -> p k n", n=w.shape[-1]),
                                 w).then_inc(ew_in[slot], 16)

            def of_expert(w, e):
                return w[bass.ds(e, 1)].rearrange("o (k p) n -> p (o k) n", p=P)

            job_done(sp, J_HT - 2)
            job_done(sp, J_HT - 1)
            load_weights(0, *(w.rearrange("(k p) n -> p k n", p=P) for w in (sg, su, sd)))
            load_weights(1, *(of_expert(w, 0) for w in (wg, wu, wd)))
            for g in range(NT // 4):
                sp.wait_ge(h_ready, g + 1)
                sp.dma_start(hrows[g * 4 * P:(g + 1) * 4 * P, :].rearrange("(t p) d -> p t d", p=P),
                             h_sb[:, g * 4:(g + 1) * 4, :]).then_inc(hrows_out, 16)
            with sp.Fori(0, NCHUNK) as c:
                for half in range(2):
                    for i in range(2):
                        job_done(sp, J_SHARED + half * 2 + i, c * 2)
                    sp.dma_start(acc[bass.ds(c * 512 + half * 256, 256), :].rearrange("(t p) d -> p t d", p=P),
                                 sacc[:, half * 2:half * 2 + 2, :]).then_inc(sacc_out[half], 16)
            sp.wait_ge(tbl_out, 16 * NT * TOPK)

            def load_ids(dst, e, done):
                sp.dma_start(dst[0:CROWS, 0:CTL - 1, :],
                             tbl[bass.ds(e * CAP, (CTL - 1) * CROWS), :].rearrange("(c p) w -> p c w", p=CROWS))\
                  .then_inc(done, 16)
                lo, rows = CAP_TILES[-1]
                sp.dma_start(dst[0:rows, CTL - 1, :], tbl[bass.ds(e * CAP + lo, rows), :]).then_inc(done, 16)

            def feed(par, turn, weights):
                e = turn * 2 + par
                sp.wait_ge(job_ready[1], (J_EXPERT // 2 - 2 + 1) + e)
                load_ids(ids_g[:, par], e, idg_in[par])
                if weights:
                    sp.wait_ge(w_lo_done, e * WPIECES)
                    load_weights((par + 1) % 2, *(of_expert(w, e) for w in (wg, wu, wd)))
                sp.wait_ge(ysb_free, e + 1)
                load_ids(ids_s[:, par], e, ids_in[par])

            feed(0, 0, False)
            feed(1, 0, True)
            with sp.Fori(1, E // 2) as i:
                feed(0, i, True)
                feed(1, i, True)
            sp.wait_ge(add_out, 16 * CTL * E)
            sp.dma_start(out.rearrange("b s d -> (b s) d"), acc[0:NTOK, :]).then_inc(final_out, 16)
            sp.wait_ge(final_out, 16)

        @block.gpsimd
        def _(pool):
            seq = Chain(pool, pool_seq)
            seq.done(pool.memset(zeros[:, :], 0.0))
            seq.done(pool.memset(tinit[:, :, :].bitcast(F32), 0.0))
            seq.done(pool.memset(ident[:, :], 0.0))
            seq.done(pool.memset(lower[:, :], 1.0))
            seq.done(pool.memset(ones[:, :], 1.0))
            seq.done(pool.memset(eps[:, :], EPS))
            seq.wait()
            seq.done(pool.iota(tinit[:, :, 0], pattern=[[1, CAP]], base=NTOK, channel_multiplier=0))
            seq.done(pool.affine_select(out=ident[:, :], in_=ident[:, :], compare_op=ALU.not_equal, fill=1.0,
                                        base=0, pattern=[[-1, P]], channel_multiplier=1))
            seq.done(pool.affine_select(out=lower[:, :], in_=lower[:, :], compare_op=ALU.is_gt, fill=0.0,
                                        base=0, pattern=[[1, P]], channel_multiplier=-1))
            seq.done(pool.iota(iota_e[:, :], pattern=[[1, E]], base=0, channel_multiplier=0,
                               allow_small_or_imprecise_dtypes=True))
            seq.done(pool.iota(dropslot[:, :, :], pattern=[[P * TOPK, NT], [1, TOPK]], base=SLOTS,
                               channel_multiplier=TOPK, allow_small_or_imprecise_dtypes=True))
            for k in range(TOPK):
                seq.done(pool.iota(entry[:, :, k, 0], pattern=[[P, NT]], base=0, channel_multiplier=1))
            seq.wait()
            pool.sem_inc(consts, 2)
            seq.done(pool.memset(mask4[:, :, :], 0.0))
            seq.wait()
            for base in (0, -DH):
                seq.done(pool.affine_select(out=mask4[:, :, :], in_=mask4[:, :, :], compare_op=ALU.not_equal,
                                            fill=1.0, base=base, pattern=[[-1, 4], [0, P]], channel_multiplier=1))
                seq.wait()
            seq.done(pool.tensor_copy(ident4[:, :, :], ident[:, :].unsqueeze(1).broadcast_to([P, 4, P])))
            for part, value in [
                    (part.bitcast(F32), value) for h in range(2)
                    for part, value in ((neg[h], 0.0), (k1[h][:, KEYS:KEYS + 1], 0.0), (k2[h][OTHER[h], :], 0.0),
                                        (q2[h][OTHER[h], :], 0.0), (k2[h][MROW[h], :], 1.0))]:
                seq.done(pool.memset(part, value))
                seq.wait()
            pool.sem_inc(pair_consts, 1)
            pool.wait_ge(kv_ready, 1)
            seq.done(pool.memset(vals[:, :, :, :, :], 1.0))
            seq.wait()
            pool.sem_inc(ones_ready, 1)
            for k in range(DT):
                pool.wait_ge(kv_hi, DT + k + 1)
                pool.tensor_tensor(kvT_lo[:, k, KEYS:], kvT[:, k, KEYS:], kvT_hi[:, k, KEYS:].bitcast(F32),
                                   ALU.subtract).then_inc(kv_split[1], 1)
            pool.sem_inc(ysb_free, 2)

            def attend(events, pair, end=False):
                for ev, back in events:
                    hp = pair - back
                    if ev[0] == "k" and ev[2] == 2:
                        b = ev[1]
                        pool.wait_ge(pair_hi, hp * HI_HP + (b + 1) * 5)
                        pool.sem_inc(pool_step, 1)
                        for h in range(2):
                            pool.dma_start(k2[h][ROWK[h], 0:KEYS], k1[h][ROWK[h], 0:KEYS])\
                                .then_inc(copies_in[b], 16)
                            pool.dma_start(q1[h][OTHER[h], :], q1[h][ROWK[h], :]).then_inc(copies_in[b], 16)
                    if ev[0] == "norm":
                        pool.wait_ge(rinv_ready, hp * (O_HP // 2) + ev[1] // 2 + 1)
                        pool.tensor_tensor(oT[:, :], oT[:, :], rinv[:, :], ALU.mult).then_inc(o_normed, 1)

            attend(FIRST, 0)
            with pool.Fori(1, HP) as hp:
                attend(PAIR, hp)
            attend(END, HP - 1, end=True)

            for piece in range(WPIECES):
                c = slice(piece * 3 * W // WPIECES, (piece + 1) * 3 * W // WPIECES)
                pool.wait_ge(w_hi_done, piece + 1)
                pool.tensor_tensor(ws_lo[0][:, c], w_raw[0][:, c], ws_hi[0][:, c].bitcast(F32),
                                   ALU.subtract).then_inc(w_lo_done, 1)
            pool.wait_ge(init_out, 48)
            pool.wait_ge(slots_ready, 1)
            for t in range(NT):
                for k in range(TOPK):
                    pool.indirect_dma_start(
                        out=tbl[:, :],
                        out_offset=bass.IndirectOffsetOnAxis(ap=slot[:, t, k:k + 1].bitcast(U32), axis=0),
                        in_=entry[:, t, k, :], in_offset=None).then_inc(tbl_out, 16)

            def gather(par, turn):
                pool.wait_ge(hrows_out, 16 * (NT // 4))
                pool.wait_ge(idg_in[par], turn * 32 + 32)
                pool.sem_inc(pool_step, 1)
                for c, (_, rows) in enumerate(CAP_TILES):
                    pool.indirect_dma_start(
                        out=xg[par][0:rows, c, :], out_offset=None, in_=hrows[:, :],
                        in_offset=bass.IndirectOffsetOnAxis(ap=ids_g[0:rows, par, c, 0:1].bitcast(U32), axis=0))\
                        .then_inc(rows_in[par], 16)

            def add(par, turn):
                e = turn * 2 + par
                pool.wait_ge(sacc_out[0], 16 * NCHUNK + 16)
                pool.wait_ge(sacc_out[1], 16 * NCHUNK + 16)
                pool.wait_ge(ysb_ready, e * CTL + CTL + 2)
                pool.sem_inc(pool_step, 1)
                for c, (_, rows) in enumerate(CAP_TILES):
                    pool.indirect_dma_start(
                        out=acc[:, :], in_=y_sb[par][0:rows, c, :], in_offset=None, compute_op=ALU.add,
                        out_offset=bass.IndirectOffsetOnAxis(ap=ids_s[0:rows, par, c, 0:1].bitcast(U32), axis=0))\
                        .then_inc(add_out, 16)
                pool.wait_ge(add_out, (e + 1) * 16 * CTL)
                pool.sem_inc(ysb_free, 1)

            gather(0, 0)
            gather(1, 0)
            with pool.Fori(0, E // 2 - 1) as i:
                gather(0, i + 1)
                add(0, i)
                gather(1, i + 1)
                add(1, i)
            add(0, E // 2 - 1)
            add(1, E // 2 - 1)

        @block.tensor
        def _(pe):
            pe.wait_ge(consts, 2)
            j = 0
            for b in range(B):
                pe.wait_ge(z_ready, b + 1)
                for k in range(DT):
                    for half in range(2):
                        bank_free(pe, j)
                        for i in range(4):
                            mm = pe.transpose(ps_t[j % 2][:, i * P:(i + 1) * P],
                                              z_sb[:, b * QT_N + half * 4 + i, k * P:(k + 1) * P], ident[:, :])
                        mm.then_inc(job_ready[j % 2], 1)
                        j += 1
            pe.wait_ge(z_ready, B + 1)
            for k in range(DT):
                bank_free(pe, j)
                for b in range(B):
                    mm = pe.transpose(ps_t[j % 2][:, b * P:b * P + CT], zc_sb[:, b, k * P:(k + 1) * P],
                                      ident[0:CT, 0:CT])
                mm.then_inc(job_ready[j % 2], 1)
                j += 1
            assert j == JOBS_A
            job_done(pe, j - 2)
            job_done(pe, j - 1)

            def product(ps, pairs):
                for n, (a, m) in enumerate(pairs):
                    mm = pe.matmul(ps, a, m, start=(n == 0), stop=(n == len(pairs) - 1))
                return mm

            def split_pairs(a_hi, a_lo, m_hi, m_lo):
                return [(a_hi, m_hi), (a_hi, m_lo), (a_lo, m_hi)]

            pe.wait_ge(pair_consts, 1)
            pe.wait_ge(ones_ready, 1)
            pe.wait_ge(wout_in, 16)

            def attend(events, pair, end=False):
                for ev, back in events:
                    kind, a = ev[0], ev[1]
                    hp = pair - back
                    more = (pair + end) * (JOBS_HP // 2)
                    if kind == "cen" or ev in RING:
                        jn = job_of(ev, end)
                        bank = ps_t[jn % 2]
                        bank_free(pe, jn, more)
                    if kind in "kq":
                        if ev == ("k", 0, 0):
                            pe.wait_ge(w_split, hp + 1)
                        if ev == ("k", a, 0):
                            pe.wait_ge(kv_split[a], DT)
                        lo, w = ((0, 512), (512, 512), (S, CT))[ev[2]]
                        lo += a * KEYS
                        c = int(kind == "k")
                        if w == CT:
                            pairs = [(w_hp[:, k, c, :], kvT[:, k, lo:lo + w]) for k in range(DT)]
                        else:
                            pairs = [p for k in range(DT)
                                     for p in split_pairs(w_hi[:, k, c, :], w_lo[:, k, c, :],
                                                          kvT_hi[:, k, lo:lo + w], kvT_lo[:, k, lo:lo + w])]
                        product(bank[:, 0:w], pairs).then_inc(job_ready[jn % 2], 1)
                    if kind == "v":
                        for s_, t in enumerate(((0, 1, 2, 3), (4, 5, 6, 7), (8,))[ev[2]]):
                            rows = P if t < QT_N else CT
                            lo = a * KEYS + t * P
                            mm = product(bank[0:rows, s_ * P:(s_ + 1) * P],
                                         [(kvT[:, k, lo:lo + rows], w_hp[:, k, 2, :]) for k in range(DT)])
                        mm.then_inc(job_ready[jn % 2], 1)
                    if kind == "max":
                        b, h, half = a // QUADS, a % 2, a % QUADS // 2
                        if h == 0 and ev[2] == 0:
                            pe.wait_ge(pair_hi, hp * HI_HP + b * 5 + 4 + half)
                        pe.wait_ge(max_done, hp * MAX_HP + a * 4 + ev[2] + 1)
                        c = half * 512 + ev[2] * P
                        for lo, w in ((0, 512), (512, 512), (S, CT + 1)):
                            mm = pe.matmul(scores_m[:, lo:lo + w], q1[h][ROWK[h], c:c + P],
                                           k1[h][ROWK[h], lo:lo + w], start=True, stop=True)
                        mm.then_inc(max_ready, 1)
                    if kind == "row":
                        pe.wait_ge(max_done, hp * MAX_HP + a * 4 + 4 + 1)
                        pe.matmul(bank[:, :], neg[a % 2], ident4[:, :, :].rearrange("p a n -> p (a n)"),
                                  start=True, stop=True).then_inc(job_ready[jn % 2], 1)
                    if kind == "st":
                        b, h, c, kt = a // QUADS, a % 2, a % QUADS // 2 * 512, ev[2]
                        n = a * KT_N + kt
                        rows = P if kt < QT_N else CT
                        r = slice(kt * P, kt * P + rows)
                        kr = slice(0, K2ROWS[h])
                        if kt == 0 and a % QUADS == 0:
                            pe.wait_ge(copies_in[b], hp * 64 + 64)
                            job_done(pe, job_of(("q", b, 0)), more)
                            job_done(pe, job_of(("q", b, 1)), more)
                        pe.wait_ge(exp_done, hp * ST_HP + n + 1)
                        pe.matmul(ps_st[0:rows, n % 2, :], k1[h][:, r], q1[h][:, c:c + 512],
                                  start=True, stop=False)
                        if kt == 0:
                            job_done(pe, job_of(("row", a)), more)
                        pe.matmul(ps_st[0:rows, n % 2, :], k2[h][kr, r], q2[h][kr, c:c + 512],
                                  start=False, stop=True).then_inc(st_ready, 1)
                    if kind == "av":
                        kt = ev[2]
                        if kt == 0:
                            pe.wait_ge(o_free, hp * O_HP + a + 1)
                            job_done(pe, job_of(("v", a // QUADS, 1)), hp * (JOBS_HP // 2))
                            job_done(pe, job_of(("v", a // QUADS, 2)), hp * (JOBS_HP // 2))
                        pe.wait_ge(exp_done, hp * ST_HP + a * KT_N + kt + 1 + 2)
                        rows = P if kt < QT_N else CT
                        mm = pe.matmul(ps_o[:, :], vals[0:rows, a // QUADS, kt, a % 2, :], probsT[0:rows, a % 2, kt, :],
                                       start=(kt == 0), stop=(kt == KT_N - 1))
                        if kt == KT_N - 1:
                            mm.then_inc(o_ready, 1)
                    if kind == "cen":
                        pe.wait_ge(z_ready, B + 2)
                        pe.transpose(bank[:, 0:GE], cen[:, a * P:(a + 1) * P], ident[0:GE, 0:GE])\
                          .then_inc(job_ready[jn % 2], 1)
                    if kind == "out":
                        pe.wait_ge(o_normed, hp * (O_HP // 2) + a // 2 + 1)
                        for i in range(2):
                            c = (ev[2] * 2 + i) * P
                            mm = pe.matmul(bank[:, i * D:(i + 1) * D], oT[:, c:c + P],
                                           wout_sb[:, bass.ds(hp, 1), :].rearrange("p o n -> p (o n)"),
                                           start=True, stop=True)
                        mm.then_inc(job_ready[jn % 2], 1)

            pe.wait_ge(w_in, 48)
            attend(FIRST, 0)
            with pe.Fori(1, HP) as hp:
                attend(PAIR, hp)
            attend(END, HP - 1, end=True)

            j = J_HT

            def turn_h(g):
                nonlocal j
                pe.wait_ge(h_ready, g + 1)
                for k in range(DT):
                    bank_free(pe, j)
                    for i in range(4):
                        mm = pe.transpose(ps_t[j % 2][:, i * P:(i + 1) * P],
                                          h_sb[:, g * 4 + i, k * P:(k + 1) * P], ident[:, :])
                    mm.then_inc(job_ready[j % 2], 1)
                    j += 1

            def score(g):
                for k in range(DT):
                    job_done(pe, J_HT + g * DT + k)
                for t in range(g * 4, g * 4 + 4):
                    lo = (t % 8) * GE
                    for k in range(DT):
                        mm = pe.matmul(router_bank[t // 8][:, lo:lo + GE], hT[:, k, t * P:(t + 1) * P],
                                       cT[:, k, :], start=(k == 0), stop=(k == DT - 1))
                mm.then_inc(router_ready, 1)

            router_bank = (ps_m[:, 2, :], ps_o)
            for g in range(NT // 4):
                turn_h(g)
                if g:
                    score(g - 1)
            assert j == J_SHARED
            score(NT // 4 - 1)
            pe.wait_ge(chosen_ready, 1)
            pe.matmul(ps_o[:, :], lower[:, :], chosen[:, :, :].rearrange("p t e -> p (t e)"), start=True, stop=False)
            pe.matmul(ps_o[:, :], ones[:, :], before[:, :, :].rearrange("p t e -> p (t e)"), start=False, stop=True)\
              .then_inc(pos_ready, 1)

            def up(slot, width, x_hi, x_lo, g0):
                for ht in range(HT):
                    pe.wait_ge(gu_free, g0 + ht + 1)
                    c = slice(ht * P, (ht + 1) * P)
                    for i, bank in enumerate((ps_m, ps_st)):
                        w_h, w_l = gate_up(ws_hi[slot], i), gate_up(ws_lo[slot], i)
                        mm = product(bank[:, ht % 2, 0:width],
                                     [p for k in range(DT)
                                      for p in split_pairs(w_h[:, k, c], w_l[:, k, c], x_hi(k), x_lo(k))])
                    mm.then_inc(gu_ready, 1)

            def down(slot, tiles, banks, g0, claim, done):
                d_h, d_l = down_of(ws_hi[slot]), down_of(ws_lo[slot])
                order = [(k, c) for k in range(HT) for c in range(2)]
                order += [(k, c) for c in range(2, len(tiles)) for k in range(HT)]
                for k, c in order:
                    lo, rows = tiles[c]
                    if k == 0:
                        claim(c)
                    if c == 0:
                        pe.wait_ge(hid_done, g0 + k + 1 + 2)
                    for n, (a, m) in enumerate(split_pairs(hid_hi[:, k, lo:lo + rows], hid_lo[:, k, lo:lo + rows],
                                                           d_h[:, k, :], d_l[:, k, :])):
                        mm = pe.matmul(banks[c], a, m, start=(k == 0 and n == 0), stop=(k == HT - 1 and n == 2))
                    if k == HT - 1:
                        mm.then_inc(done[c], 1)

            pe.wait_ge(w_lo_done, WPIECES)
            with pe.Fori(0, NCHUNK) as c:
                up(0, 512, lambda k: hT_hi[:, k, bass.ds(c * 512, 512)],
                   lambda k: hT_lo[:, k, bass.ds(c * 512, 512)], c * HT)
                down(0, [(i * P, P) for i in range(4)], [ps_t[i % 2][:, 0:D] for i in range(4)], c * HT,
                     lambda i: bank_free(pe, J_SHARED + i, c * 2), [job_ready[i % 2] for i in range(4)])

            def turn_rows(par, turn):
                pe.wait_ge(rows_in[par], turn * (16 * CTL) + 16 * CTL)
                for k in range(DT):
                    jj = J_EXPERT + par * DT + k
                    bank_free(pe, jj, turn * DT)
                    for c, (lo, rows) in enumerate(CAP_TILES):
                        mm = pe.transpose(ps_t[jj % 2][:, lo:lo + rows], xg[par][0:rows, c, k * P:(k + 1) * P],
                                          ident[0:rows, 0:rows])
                    mm.then_inc(job_ready[jj % 2], 1)

            def expert_up(par, turn):
                e = turn * 2 + par
                pe.wait_ge(w_lo_done, e * WPIECES + 2 * WPIECES - 1)
                for k in range(DT):
                    job_done(pe, J_EXPERT + par * DT + k, turn * DT)
                up((par + 1) % 2, CAP, lambda k: xe_hi[:, k, :], lambda k: xe_lo[:, k, :],
                   NCHUNK * HT + turn * (2 * HT) + par * HT)

            def expert_down(par, turn):
                pe.wait_ge(w_lo_done, turn * (2 * WPIECES) + (par + 2) * WPIECES)
                y0 = turn * (2 * CTL) + par * CTL
                down((par + 1) % 2, CAP_TILES,
                     [ey_bank[(par * CTL + c) % 2][0:rows, 0:D] for c, (_, rows) in enumerate(CAP_TILES)],
                     NCHUNK * HT + turn * (2 * HT) + par * HT,
                     lambda c: pe.wait_ge(ysb_ready, y0 + c + 1), [ey_ready] * CTL)

            turn_rows(0, 0)
            with pe.Fori(0, E // 2 - 1) as i:
                expert_up(0, i)
                turn_rows(1, i)
                expert_down(0, i)
                expert_up(1, i)
                turn_rows(0, i + 1)
                expert_down(1, i)
            last = E // 2 - 1
            expert_up(0, last)
            turn_rows(1, last)
            expert_down(0, last)
            expert_up(1, last)
            expert_down(1, last)

        @block.vector
        def _(dve):
            seq = Chain(dve, dve_seq)
            for s in job_free:
                dve.sem_inc(s, 1)
            dve.sem_inc(o_free, 1)
            dve.sem_inc(max_done, 1)
            dve.sem_inc(gu_free, 2)
            dve.sem_inc(hid_done, 2)
            for s in sacc_out:
                dve.sem_inc(s, 16)

            def spread(src, sts, lo, n, rows=P):
                for t in range(n):
                    seq.done(dve.bn_stats(sts[0:rows, t, :], src[0:rows, t, :]))
                seq.wait()
                for t in range(n):
                    ins = dve.bn_aggr(mv[0:rows, lo + t, :], sts[0:rows, t, :])
                    seq.done(ins)
                seq.wait()

            def normed(dst, src, lo, n, rows=P):
                seq.done(dve.reciprocal(rstd[0:rows, lo:lo + n], std[0:rows, lo:lo + n]))
                seq.wait()
                scaled(dst, src, lo, n, rows)

            def scaled(dst, src, lo, n, rows=P):
                for t in range(n):
                    seq.done(dve.tensor_scalar(dst[0:rows, t, :], src[0:rows, t, :], mv[0:rows, lo + t, 0:1],
                                               rstd[0:rows, lo + t:lo + t + 1], ALU.subtract, ALU.mult))
                seq.wait()

            dve.wait_ge(x_in, 16 * B)
            tiles = [slice(b * QT_N, (b + 1) * QT_N) for b in range(B)]
            for b in range(B):
                spread(x_sb[:, tiles[b], :], stats, b * QT_N, QT_N)
                dve.sem_inc(var_ready, 1)
            for b in range(B):
                t = tiles[b]
                dve.wait_ge(std_ready, b + 1)
                seq.done(dve.reciprocal(rstd[:, t], std[:, t]))
                seq.wait()
                for _ in range(2):
                    seq.done(dve.tensor_tensor(mv[:, t, 1], mv[:, t, 1], rstd[:, t], ALU.mult))
                    seq.wait()
                dve.sem_inc(var_ready, 1)
            for b in range(B):
                t = tiles[b]
                dve.wait_ge(std_ready, B + b + 1)
                seq.done(dve.reciprocal(std[:, t], std[:, t]))
                seq.wait()
                seq.done(dve.tensor_tensor(rstd[:, t], rstd[:, t], std[:, t], ALU.mult))
                seq.wait()
                scaled(z_sb[:, t, :], x_sb[:, t, :], b * QT_N, QT_N)
                dve.sem_inc(z_ready, 1)
            nv = 2 * B
            dve.wait_ge(small_in, 16 * 8)
            for b in range(B):
                for k in range(DT):
                    jj = b * DT * 2 + k * 2
                    job_filled(dve, jj)
                    dve.tensor_scalar(kvT[:, k, b * KEYS:b * KEYS + 512], ps_t[jj % 2][:, :], gb[:, 0, k:k + 1],
                                      gb[:, 1, k:k + 1], ALU.mult, ALU.add).then_inc(job_free[jj % 2], 1)
            spread(ctx_sb, cstats, NT, B, CT)
            dve.sem_inc(var_ready, 1)
            nv += 1
            dve.wait_ge(std_ready, nv)
            normed(zc_sb, ctx_sb, NT, B, CT)
            dve.sem_inc(z_ready, 1)
            for k in range(DT):
                jj = B * DT * 2 + k
                job_filled(dve, jj)
                dve.tensor_scalar(kvT[:, k, :].rearrange("p (b n) -> p b n", b=B)[:, :, S:KEYS],
                                  ps_t[jj % 2][:, 0:B * P].rearrange("p (b n) -> p b n", b=B)[:, :, 0:CT],
                                  gb[:, 2, k:k + 1], gb[:, 3, k:k + 1], ALU.mult, ALU.add)\
                   .then_inc(job_free[jj % 2], 1)
            job_done(dve, B * DT * 2 + DT - 2)
            job_done(dve, B * DT * 2 + DT - 1)
            dve.sem_inc(kv_ready, 1)
            for k in range(DT):
                dve.wait_ge(kv_hi, k + 1)
                dve.tensor_tensor(kvT_lo[:, k, 0:KEYS], kvT[:, k, 0:KEYS], kvT_hi[:, k, 0:KEYS].bitcast(F32),
                                  ALU.subtract).then_inc(kv_split[0], 1)
            dve.wait_ge(std_ready, nv + 1)
            seq.done(dve.tensor_scalar(cstat[:, 2:3], cstat[:, 1:2], 1e-12, None, ALU.max))
            seq.wait()
            seq.done(dve.reciprocal(cstat[:, 3:4], cstat[:, 2:3]))
            seq.wait()
            seq.done(dve.tensor_scalar(cen[:, :], cen[:, :], cstat[:, 3:4], None, ALU.mult))
            seq.wait()
            dve.sem_inc(z_ready, 1)

            dve.wait_ge(pair_consts, 1)

            def attend(events, pair, end=False):
                for ev, back in events:
                    kind, a = ev[0], ev[1]
                    hp = pair - back
                    more = (pair + end) * (JOBS_HP // 2)
                    if kind == "cen" or ev in RING:
                        jn = job_of(ev, end)
                        bank, free = ps_t[jn % 2], job_free[jn % 2]
                    if kind == "w":
                        dve.wait_ge(w_hi_ready, hp + 1)
                        dve.tensor_tensor(w_lo[:, :, :, :], w_hp[:, :, 0:2, :], w_hi[:, :, :, :].bitcast(F32),
                                          ALU.subtract).then_inc(w_split, 1)
                    if kind in "kq":
                        lo, w = ((0, 512), (512, 512), (S, CT))[ev[2]]
                        dve.wait_ge(pair_hi, hp * HI_HP + a * 5 + PROJECT.index((kind, ev[2])) + 1)
                        for h in range(2):
                            if kind == "k":
                                ins = dve.tensor_tensor(k1[h][OTHER[h], lo:lo + w], bank[ROWK[h], 0:w],
                                                        k1[h][ROWK[h], lo:lo + w].bitcast(F32), ALU.subtract)
                            else:
                                ins = dve.scalar_tensor_tensor(q2[h][ROWK[h], lo:lo + w], bank[ROWK[h], 0:w],
                                                               DH ** -0.5, q1[h][ROWK[h], lo:lo + w].bitcast(F32),
                                                               ALU.mult, ALU.subtract)
                        ins.then_inc(free, 1)
                    if kind == "max":
                        dve.wait_ge(max_ready, hp * MAX_HP + a * 4 + ev[2] + 1)
                        c = MROW[a % 2].start + ev[2]
                        dve.tensor_reduce(neg[a % 2][:, c:c + 1], scores_m[:, 0:KEYS], AX.X, ALU.max, negate=True)\
                           .then_inc(max_done, 1)
                    if kind == "row":
                        r = MROW[a % 2]
                        c = a % QUADS // 2 * 512
                        job_filled(dve, jn, more)
                        dve.tensor_tensor(q2[a % 2][r, c:c + 512], bank[r, :],
                                          mask4[r, :, :].rearrange("p a n -> p (a n)"), ALU.mult).then_inc(free, 1)
                    if kind == "norm":
                        dve.wait_ge(o_free, hp * O_HP + a + 2)
                        dve.reciprocal(rinv[:, :], rinv[:, :]).then_inc(rinv_ready, 1)
                    if kind == "cen":
                        job_filled(dve, jn, more)
                        dve.tensor_copy(cT[:, a, :], bank[:, 0:GE]).then_inc(free, 1)
                    if kind == "out":
                        t = a // QUADS * QT_N + a % QUADS // 2 * 4 + ev[2] * 2
                        job_filled(dve, jn, more)
                        dve.tensor_tensor(x_sb[:, t:t + 2, :], x_sb[:, t:t + 2, :],
                                          bank[:, :].rearrange("p (t n) -> p t n", t=2), ALU.add).then_inc(free, 1)

            attend(FIRST, 0)
            with dve.Fori(1, HP) as hp:
                attend(PAIR, hp)
            attend(END, HP - 1, end=True)

            def weights_lo(slot, idx, piece):
                c = slice(piece * 3 * W // WPIECES, (piece + 1) * 3 * W // WPIECES)
                dve.wait_ge(w_hi_done, idx + 1)
                dve.tensor_tensor(ws_lo[slot][:, c], w_raw[slot][:, c], ws_hi[slot][:, c].bitcast(F32),
                                  ALU.subtract).then_inc(w_lo_done, 1)

            job_done(dve, J_HT - 2)
            job_done(dve, J_HT - 1)
            def norm_h(g):
                dve.wait_ge(std_ready, nv + 1 + g + 1)
                normed(h_sb[:, g * 4:g * 4 + 4, :], x_sb[:, g * 4:g * 4 + 4, :], g * 4, 4)
                dve.sem_inc(h_ready, 1)

            def low_h(g):
                for k in range(DT):
                    jn = J_HT + g * DT + k
                    c = slice(g * 512, (g + 1) * 512)
                    dve.wait_ge(h_hi, g * DT + k + 1)
                    dve.tensor_tensor(hT_lo[:, k, c], ps_t[jn % 2][:, :], hT_hi[:, k, c].bitcast(F32), ALU.subtract)\
                       .then_inc(job_free[jn % 2], 1)

            for g in range(NT // 4):
                spread(x_sb[:, g * 4:g * 4 + 4, :], stats[:, g * 4:g * 4 + 4, :], g * 4, 4)
                dve.sem_inc(var_ready, 1)
                if g:
                    norm_h(g - 1)
                if g > 1:
                    low_h(g - 2)
            norm_h(NT // 4 - 1)
            for g in range(NT // 4 - 2, NT // 4):
                low_h(g)
            dve.wait_ge(norm_ready, 1)
            seq.done(dve.tensor_scalar(rnorm[:, :], rnorm[:, :], 1e-12, None, ALU.max))
            seq.wait()
            seq.done(dve.reciprocal(ssq[:, :], rnorm[:, :]))
            seq.wait()
            dve.wait_ge(router_ready, NT // 4)
            for half, bank in enumerate((ps_m[:, 2, 0:8 * GE], ps_o[:, 0:8 * GE])):
                seq.done(dve.tensor_tensor(sc[:, half * 8:half * 8 + 8, :],
                                           bank.rearrange("p (t g) -> p t g", t=8),
                                           ssq[:, half * 8:half * 8 + 8].unsqueeze(2).broadcast_to([P, 8, GE]),
                                           ALU.mult))
            seq.wait()

            def top4(src, width):
                for t in range(NT):
                    seq.done(dve.max(top8[:, t, :], src[:, t, 0:width]))
                seq.wait()
                for t in range(NT):
                    seq.done(dve.max_index(top8i[:, t, :], top8[:, t, :], src[:, t, 0:width]))
                seq.wait()
                seq.done(dve.tensor_copy(topf[:, :, :], top8i[:, :, 0:TOPK]))
                seq.wait()

            def hot(dst, width):
                seq.done(dve.tensor_tensor(dst, topf[:, :, :].unsqueeze(3).broadcast_to([P, NT, TOPK, width]),
                                           iota_e[:, 0:width].unsqueeze(1).unsqueeze(1)
                                           .broadcast_to([P, NT, TOPK, width]), ALU.is_equal))
                seq.wait()

            dve.wait_ge(consts, 2)
            top4(sc, G)
            gh = picked[:, :, :, 0:G]
            hot(gh, G)
            seq.done(dve.tensor_reduce(gmask[:, :, :], gh.rearrange("p t k g -> p t g k"), AX.X, ALU.add))
            seq.done(dve.tensor_tensor(sc[:, :, G:GE], sc[:, :, G:GE],
                                       bias_bc[:, :].unsqueeze(1).broadcast_to([P, NT, E]), ALU.add))
            seq.wait()
            m4 = masked[:, :, :].rearrange("p t (g i) -> p t g i", i=PER_G)
            seq.done(dve.tensor_tensor(m4, sc[:, :, G:GE].rearrange("p t (g i) -> p t g i", i=PER_G),
                                       gmask[:, :, :].unsqueeze(3).broadcast_to([P, NT, G, PER_G]), ALU.mult))
            seq.wait()
            seq.done(dve.tensor_scalar(gmask[:, :, :], gmask[:, :, :], -1.0, 1e9, ALU.add, ALU.mult))
            seq.wait()
            seq.done(dve.tensor_tensor(m4, m4, gmask[:, :, :].unsqueeze(3).broadcast_to([P, NT, G, PER_G]), ALU.add))
            seq.wait()
            top4(masked, E)
            seq.done(dve.tensor_tensor(keep[:, :, :], top8[:, :, 0:TOPK], top8[:, :, 0:1].broadcast_to([P, NT, TOPK]),
                                       ALU.subtract))
            seq.wait()
            dve.sem_inc(gate_in, 1)
            hot(onehot[:, :, :, :], E)
            seq.done(dve.tensor_reduce(chosen[:, :, :], onehot[:, :, :, :].rearrange("p t k e -> p t e k"),
                                       AX.X, ALU.add))
            seq.done(dve.memset(before[:, 0, :], 0.0))
            seq.wait()
            for t in range(1, NT):
                seq.done(dve.tensor_tensor(before[:, t, :], before[:, t - 1, :], chosen[:, t - 1, :], ALU.add))
                seq.wait()
            dve.sem_inc(chosen_ready, 1)
            dve.wait_ge(gate_exp, 1)
            seq.done(dve.tensor_reduce(gsum[:, :], posk[:, :, :], AX.X, ALU.add))
            seq.wait()
            seq.done(dve.reciprocal(gsum[:, :], gsum[:, :]))
            seq.wait()
            seq.done(dve.tensor_tensor(entry[:, :, :, 1].bitcast(F32), posk[:, :, :],
                                       gsum[:, :].unsqueeze(2).broadcast_to([P, NT, TOPK]), ALU.mult))
            seq.wait()
            dve.wait_ge(pos_ready, 1)
            seq.done(dve.tensor_tensor(picked[:, :, :, :], onehot[:, :, :, :],
                                       ps_o[:, :].rearrange("p (t e) -> p t e", t=NT).unsqueeze(2)
                                       .broadcast_to([P, NT, TOPK, E]), ALU.mult))
            seq.wait()
            seq.done(dve.tensor_reduce(posk[:, :, :], picked[:, :, :, :], AX.X, ALU.add))
            seq.wait()
            seq.done(dve.tensor_scalar(keep[:, :, :], posk[:, :, :], float(CAP), None, ALU.is_lt))
            seq.done(dve.tensor_scalar(topf[:, :, :], topf[:, :, :], float(CAP), None, ALU.mult))
            seq.wait()
            seq.done(dve.tensor_tensor(posk[:, :, :], posk[:, :, :], topf[:, :, :], ALU.add))
            seq.wait()
            seq.done(dve.tensor_tensor(posk[:, :, :], posk[:, :, :], dropslot[:, :, :], ALU.subtract))
            seq.wait()
            seq.done(dve.tensor_tensor(posk[:, :, :], posk[:, :, :], keep[:, :, :], ALU.mult))
            seq.wait()
            seq.done(dve.tensor_tensor(slot[:, :, :], posk[:, :, :], dropslot[:, :, :], ALU.add))
            seq.wait()
            dve.sem_inc(slots_ready, 1)

            def hidden(g0, width, between=None):
                def low(ht):
                    dve.wait_ge(hid_hi_done, g0 + ht + 1)
                    dve.tensor_tensor(hid_lo[:, ht, 0:width], hid32[ht % 2][:, 0:width],
                                      hid_hi[:, ht, 0:width].bitcast(F32), ALU.subtract).then_inc(hid_done, 1)

                for ht in range(HT):
                    dve.wait_ge(hid_done, g0 + ht + 1)
                    dve.wait_ge(silu_done, g0 + ht + 1)
                    dve.tensor_tensor(hid32[ht % 2][:, 0:width], silu[ht % 2][:, 0:width],
                                      ps_st[:, ht % 2, 0:width], ALU.mult).then_inc(gu_free, 1)
                    if ht:
                        low(ht - 1)
                    if between:
                        between(ht)
                low(HT - 1)

            dve.wait_ge(hrows_out, 16 * (NT // 4))
            with dve.Fori(0, NCHUNK) as c:
                hidden(c * HT, 512)
                for i in range(4):
                    jn = J_SHARED + i
                    job_filled(dve, jn, c * 2)
                    if i % 2 == 0:
                        dve.wait_ge(sacc_out[i // 2], c * 16 + 16)
                    dve.tensor_tensor(sacc[:, i, :], ps_t[jn % 2][:, 0:D],
                                      x_sb[:, bass.ds(c * 4 + i, 1), :].rearrange("p o d -> p (o d)"),
                                      ALU.add).then_inc(job_free[jn % 2], 1)

            def rows_lo(par, turn):
                for k in range(DT):
                    jn = J_EXPERT + par * DT + k
                    dve.wait_ge(xe_hi_done, turn * (2 * DT) + par * DT + k + 1)
                    dve.tensor_tensor(xe_lo[:, k, :], ps_t[jn % 2][:, 0:CAP], xe_hi[:, k, :].bitcast(F32),
                                      ALU.subtract).then_inc(job_free[jn % 2], 1)

            def expert(par, turn, more=True):
                n = turn * (2 * WPIECES) + (par + 2) * WPIECES
                hidden(NCHUNK * HT + turn * (2 * HT) + par * HT, CAP,
                       (lambda ht: ht < 2 and weights_lo(par, n + ht, ht)) if more else None)
                if more:
                    rows_lo((par + 1) % 2, turn + par)
                    for piece in range(2, WPIECES):
                        weights_lo(par, n + piece, piece)

            for piece in range(WPIECES):
                weights_lo(1, WPIECES + piece, piece)
            rows_lo(0, 0)
            with dve.Fori(0, E // 2 - 1) as i:
                expert(0, i)
                expert(1, i)
            expert(0, E // 2 - 1)
            expert(1, E // 2 - 1, False)

        @block.scalar
        def _(act):
            act.sem_inc(ysb_ready, 2)
            act.wait_ge(consts, 2)

            def root(n, lo, cnt, rows=P):
                act.wait_ge(var_ready, n)
                act.activation(std[0:rows, lo:lo + cnt], mv[0:rows, lo:lo + cnt, 1], ACT.Sqrt, bias=eps[0:rows, :])\
                   .then_inc(std_ready, 1)

            roots = 2 * B + 1
            for i in range(2):
                for b in range(B):
                    root(i * B + b + 1, b * QT_N, QT_N)
            act.wait_ge(small_in, 16 * 8)
            for b in range(B):
                for k in range(DT):
                    jn = b * DT * 2 + k * 2 + 1
                    job_filled(act, jn)
                    act.activation(kvT[:, k, b * KEYS + 512:b * KEYS + S], ps_t[jn % 2][:, :], ACT.Identity,
                                   scale=gb[:, 0, k:k + 1], bias=gb[:, 1, k:k + 1]).then_inc(job_free[jn % 2], 1)
            root(roots, NT, B, CT)
            for k in range(DT):
                job_done(act, B * DT * 2 + k)
            act.activation(sq_junk[0:GE, :], cen[:, :], ACT.Square, accum_out=cstat[:, 0:1]).then_inc(act_seq, 1)
            act.wait_ge(act_seq, 1)
            act.activation(cstat[:, 1:2], cstat[:, 0:1], ACT.Sqrt).then_inc(std_ready, 1)

            act.wait_ge(kv_ready, 1)
            for k in range(DT):
                act.activation(kvT_hi[:, k, 0:KEYS], kvT[:, k, 0:KEYS], ACT.Copy).then_inc(kv_hi, 1)
            act.preload_act_table(ACT.Exp)
            act.sem_inc(exp_done, 2)

            def attend(events, pair, end=False):
                for ev, back in events:
                    kind, a = ev[0], ev[1]
                    hp = pair - back
                    more = (pair + end) * (JOBS_HP // 2)
                    if kind == "w":
                        act.wait_ge(w_in, hp * 48 + 48)
                        act.activation(w_hi[:, :, :, :], w_hp[:, :, 0:2, :], ACT.Copy).then_inc(w_hi_ready, 1)
                    if kind in "kq":
                        jn = job_of(ev, end)
                        lo, w = ((0, 512), (512, 512), (S, CT))[ev[2]]
                        job_filled(act, jn, more)
                        for h in range(2):
                            ins = act.activation((k1 if kind == "k" else q1)[h][ROWK[h], lo:lo + w],
                                                 ps_t[jn % 2][ROWK[h], 0:w],
                                                 ACT.Copy, scale=1.0 if kind == "k" else DH ** -0.5)
                        ins.then_inc(pair_hi, 1)
                    if kind == "v":
                        t, n = ((0, 4), (4, 4), (8, 1))[ev[2]]
                        rows = P if t < QT_N else CT
                        jn = job_of(ev, end)
                        job_filled(act, jn, more)
                        for h in range(2):
                            ins = act.activation(vals[0:rows, a, t:t + n, h, ROWK[h]],
                                                 ps_t[jn % 2][0:rows, 0:n * P]
                                                 .rearrange("p (t h d) -> p h t d", t=n, h=2)[:, h], ACT.Copy)
                        ins.then_inc(job_free[jn % 2], 1)
                    if kind == "av" and ev[2] == KT_N - 1:
                        own, sums = ROWK[a % 2], OTHER[a % 2]
                        act.wait_ge(o_ready, hp * O_HP + a + 1)
                        act.activation(oT[own, :], ps_o[own, :], ACT.Copy)
                        act.activation(rinv[own, :], ps_o[sums, :], ACT.Copy).then_inc(o_free, 1)
                    if kind == "out" and ev[2] == 1:
                        job_filled(act, job_of(ev, end), more)
                    if kind == "st":
                        n = a * KT_N + ev[2]
                        rows = P if ev[2] < QT_N else CT
                        act.wait_ge(st_ready, hp * ST_HP + n + 1)
                        act.activation(probsT[0:rows, a % 2, ev[2], :], ps_st[0:rows, n % 2, :], ACT.Exp)\
                           .then_inc(exp_done, 1)

            attend(FIRST[:1], 0)
            for k in range(DT):
                act.activation(kvT_hi[:, k, KEYS:], kvT[:, k, KEYS:], ACT.Copy).then_inc(kv_hi, 1)
            attend(FIRST[1:], 0)
            with act.Fori(1, HP) as hp:
                attend(PAIR, hp)
            attend(END, HP - 1, end=True)

            for g in range(NT // 4):
                if g == 0:
                    root(roots + 1, 0, 4)
                    root(roots + 2, 4, 4)
                for k in range(DT):
                    jn = J_HT + g * DT + k
                    c = slice(g * 512, (g + 1) * 512)
                    job_filled(act, jn)
                    act.activation(hT[:, k, c], ps_t[jn % 2][:, :], ACT.Copy)
                    act.activation(hT_hi[:, k, c], ps_t[jn % 2][:, :], ACT.Copy).then_inc(h_hi, 1)
                if g < NT // 4 - 2:
                    root(roots + g + 3, (g + 2) * 4, 4)
                for t in range(g * 4, g * 4 + 4):
                    act.activation(sq_junk[:, :], h_sb[:, t, :], ACT.Square, accum_out=ssq[:, t:t + 1])\
                       .then_inc(act_seq, 1)
                    act.wait_ge(act_seq, 1 + t + 1)

            def weights_hi(slot, piece):
                c = slice(piece * 3 * W // WPIECES, (piece + 1) * 3 * W // WPIECES)
                act.activation(ws_hi[slot][:, c], w_raw[slot][:, c], ACT.Copy).then_inc(w_hi_done, 1)

            act.wait_ge(ew_in[0], 48)
            for piece in range(WPIECES):
                weights_hi(0, piece)
            act.activation(rnorm[:, :], ssq[:, :], ACT.Sqrt).then_inc(norm_ready, 1)
            act.wait_ge(gate_in, 1)
            act.activation(posk[:, :, :], keep[:, :, :], ACT.Exp).then_inc(gate_exp, 1)

            act.preload_act_table(ACT.Silu)

            def activate(g0, width, between=None):
                def high(ht):
                    act.wait_ge(gu_free, g0 + ht + 2 + 1)
                    act.activation(hid_hi[:, ht, 0:width], hid32[ht % 2][:, 0:width], ACT.Copy)\
                       .then_inc(hid_hi_done, 1)

                for ht in range(HT):
                    act.wait_ge(gu_ready, g0 + ht + 1)
                    act.activation(silu[ht % 2][:, 0:width], ps_m[:, ht % 2, 0:width], ACT.Silu)\
                       .then_inc(silu_done, 1)
                    if ht:
                        high(ht - 1)
                    if between:
                        between(ht)
                high(HT - 1)

            with act.Fori(0, NCHUNK) as c:
                activate(c * HT, 512)

            def rows_hi(par, turn):
                for k in range(DT):
                    jn = J_EXPERT + par * DT + k
                    job_filled(act, jn, turn * DT)
                    act.activation(xe_hi[:, k, :], ps_t[jn % 2][:, 0:CAP], ACT.Copy).then_inc(xe_hi_done, 1)

            def expert(par, turn, more=True):
                def first_pieces(ht):
                    if ht == 0:
                        act.wait_ge(ew_in[par], turn * 48 + 96)
                    if ht < 2:
                        weights_hi(par, ht)

                def y_out(c):
                    rows = CAP_TILES[c][1]
                    act.wait_ge(ey_ready, turn * (2 * CTL) + par * CTL + c + 1)
                    act.activation(y_sb[par][0:rows, c, :], ey_bank[(par * CTL + c) % 2][0:rows, 0:D], ACT.Copy,
                                   scale=ids_s[0:rows, par, c, 1:2].bitcast(F32)).then_inc(ysb_ready, 1)

                activate(NCHUNK * HT + turn * (2 * HT) + par * HT, CAP, first_pieces if more else None)
                if more:
                    rows_hi((par + 1) % 2, turn + par)
                    weights_hi(par, 2)
                act.wait_ge(ids_in[par], turn * 32 + 32)
                for c in range(CTL - 1):
                    y_out(c)
                if more:
                    weights_hi(par, 3)
                y_out(CTL - 1)

            act.wait_ge(hid_done, NCHUNK * HT + 2)
            act.wait_ge(job_ready[1], J_EXPERT // 2)
            act.wait_ge(ew_in[1], 48)
            for piece in range(WPIECES):
                weights_hi(1, piece)
            rows_hi(0, 0)
            with act.Fori(0, E // 2 - 1) as i:
                expert(0, i)
                expert(1, i)
            expert(0, E // 2 - 1)
            expert(1, E // 2 - 1, False)


_INS = ['x', 'ctx_1024', 'L0_xattn_ln_m_g', 'L0_xattn_ln_m_b', 'L0_xattn_ln_l_g', 'L0_xattn_ln_l_b', 'L0_xattn_Wq',
        'L0_xattn_Wkv', 'L0_xattn_Wout', 'L0_ffn_group_centroids', 'L0_ffn_expert_centroids', 'L0_ffn_bias',
        'L0_ffn_wg', 'L0_ffn_wu', 'L0_ffn_wd', 'L0_ffn_sg', 'L0_ffn_su', 'L0_ffn_sd']


def kernel(**inputs):
    import numpy as _np
    import concourse.bacc as _bacc
    from concourse import mybir as _mybir
    from concourse.bass_utils import run_bass_kernel_spmd as _run

    nc = _bacc.Bacc("TRN2", target_bir_lowering=False, num_devices=1)
    arrays, args = {}, []
    for name in _INS:
        a = _np.ascontiguousarray(inputs[name])
        arrays[f"in_{name}_dram"] = a
        args.append(nc.dram_tensor(f"in_{name}_dram", a.shape, _mybir.dt.from_np(a.dtype), kind="ExternalInput").ap())
    out = nc.dram_tensor("out_0_dram", inputs['x'].shape, F32, kind="ExternalOutput").ap()
    xattn_moe(nc, *args, out)
    r = _run(nc, [arrays], core_ids=[0])
    return r.results[0]["out_0_dram"]
```
